# Optimizing a Trainium2 kernel written in Bass

```python
import numpy as np
import jax
import jax.numpy as jnp

def _softmax(x, axis=-1):
    return jax.nn.softmax(x, axis=axis)

def _gelu(x):
    return jax.nn.gelu(x, approximate=True)

def _silu(x):
    return jax.nn.silu(x)

def _sigmoid(x):
    return jax.nn.sigmoid(x)

def _layernorm(x, axis=-1, eps=1e-05):
    m = jnp.mean(x, axis=axis, keepdims=True)
    v = jnp.var(x, axis=axis, keepdims=True)
    return (x - m) / jnp.sqrt(v + eps)

def _scatter_add(tgt, idx, src, axis=0):
    return tgt.at[idx].add(src)

def _segment_sum(src, seg, n):
    return jax.ops.segment_sum(src, seg, n)
kernel_name = 'mk_seq_postln_d1_jaxref_r8_7bf0c0'

def setup_inputs(seed: int=0):
    np.random.seed(seed)
    _w = jnp.asarray

    def _L0_attn_setup():
        import jax, jax.numpy as jnp
        import numpy as np
        DIM = 128
        H = 16
        DH = DIM // H
        K = 4
        B = 8
        N = 256
        EPS = 1e-06

        def _depthwise_conv_silu(x, w, n):
            pad = K // 2
            y = jax.lax.conv_general_dilated(x.transpose(0, 2, 1), w, window_strides=(1,), padding=[(pad, pad)], dimension_numbers=('NCH', 'OIH', 'NCH'), feature_group_count=x.shape[-1])
            y = y[..., :n]
            return jax.nn.silu(y).transpose(0, 2, 1)

        def _l2norm(x):
            return x / (jnp.linalg.norm(x, axis=-1, keepdims=True) + EPS)

        def _forward(x, Wq, bq, Wk, bk, Wv, bv, Wa, ba, Wb, bb, conv_q, conv_k, conv_v, Wo, bo):
            b_, n_, c_ = x.shape
            q = _l2norm(_depthwise_conv_silu(jax.nn.silu(x @ Wq.T + bq), conv_q, n_))
            k = _l2norm(_depthwise_conv_silu(jax.nn.silu(x @ Wk.T + bk), conv_k, n_))
            v = _depthwise_conv_silu(jax.nn.silu(x @ Wv.T + bv), conv_v, n_)
            a = jax.nn.sigmoid(x @ Wa.T + ba)
            bgate = jax.nn.sigmoid(x @ Wb.T + bb)
            q = q.reshape(b_, n_, H, DH).transpose(1, 0, 2, 3)
            k = k.reshape(b_, n_, H, DH).transpose(1, 0, 2, 3)
            v = v.reshape(b_, n_, H, DH).transpose(1, 0, 2, 3)
            a = a.transpose(1, 0, 2)
            bgate = bgate.transpose(1, 0, 2)
            S0 = jnp.zeros((b_, H, DH, DH), x.dtype)

            def step(S, inp):
                qt, kt, vt, at, bt = inp
                at = at[..., None, None]
                bt = bt[..., None, None]
                Sk = jnp.einsum('bhde,bhe->bhd', S, kt)
                outer_Sk_k = Sk[..., :, None] * kt[..., None, :]
                outer_v_k = vt[..., :, None] * kt[..., None, :]
                S_new = at * S - at * bt * outer_Sk_k + bt * outer_v_k
                ot = jnp.einsum('bhd,bhde->bhe', qt, S_new)
                return (S_new, ot)
            _, O = jax.lax.scan(step, S0, (q, k, v, a, bgate))
            O = O.transpose(1, 0, 2, 3).reshape(b_, n_, c_)
            return O @ Wo.T + bo
        key = jax.random.key(seed)
        ks = jax.random.split(key, 16)
        s = 1.0 / np.sqrt(DIM)
        d = dict(x=jax.random.normal(ks[0], (B, N, DIM), jnp.float32), Wq=jax.random.normal(ks[1], (DIM, DIM), jnp.float32) * s, bq=jnp.zeros((DIM,), jnp.float32), Wk=jax.random.normal(ks[2], (DIM, DIM), jnp.float32) * s, bk=jnp.zeros((DIM,), jnp.float32), Wv=jax.random.normal(ks[3], (DIM, DIM), jnp.float32) * s, bv=jnp.zeros((DIM,), jnp.float32), Wa=jax.random.normal(ks[4], (H, DIM), jnp.float32) * s, ba=jnp.zeros((H,), jnp.float32), Wb=jax.random.normal(ks[5], (H, DIM), jnp.float32) * s, bb=jnp.zeros((H,), jnp.float32), conv_q=jax.random.normal(ks[6], (DIM, 1, K), jnp.float32) * 0.5, conv_k=jax.random.normal(ks[7], (DIM, 1, K), jnp.float32) * 0.5, conv_v=jax.random.normal(ks[8], (DIM, 1, K), jnp.float32) * 0.5, Wo=jax.random.normal(ks[9], (DIM, DIM), jnp.float32) * s, bo=jnp.zeros((DIM,), jnp.float32))
        return d
    _L0_attn_in = _L0_attn_setup()

    def _L0_ffn_setup():
        import jax, jax.numpy as jnp
        import numpy as np
        S, B, D, H, E, K, F = (128, 4, 128, 16, 8, 2, 512)

        def _ln(x, g, b, eps=1e-05):
            mu = jnp.mean(x, axis=-1, keepdims=True)
            var = jnp.mean((x - mu) ** 2, axis=-1, keepdims=True)
            return (x - mu) * jax.lax.rsqrt(var + eps) * g + b
        key = jax.random.key(seed)
        ks = jax.random.split(key, 8)
        s = 0.02
        return {'src': jax.random.normal(ks[0], (S, B, D), jnp.float32), 'in_proj_w': jax.random.normal(ks[1], (3 * D, D), jnp.float32) * s, 'in_proj_b': jnp.zeros((3 * D,), jnp.float32), 'out_w': jax.random.normal(ks[2], (D, D), jnp.float32) * s, 'out_b': jnp.zeros((D,), jnp.float32), 'gate_w': jax.random.normal(ks[3], (E, D), jnp.float32) * s, 'gate_b': jnp.zeros((E,), jnp.float32), 'w1': jax.random.normal(ks[4], (E, F, D), jnp.float32) * s, 'b1': jnp.zeros((E, F), jnp.float32), 'w2': jax.random.normal(ks[5], (E, D, F), jnp.float32) * s, 'b2': jnp.zeros((E, D), jnp.float32), 'ln1_g': jnp.ones((D,), jnp.float32), 'ln1_b': jnp.zeros((D,), jnp.float32), 'ln2_g': jnp.ones((D,), jnp.float32), 'ln2_b': jnp.zeros((D,), jnp.float32)}
    _L0_ffn_in = _L0_ffn_setup()
    _d = {'L0_attn_x': _L0_attn_in['x'], 'L0_attn_Wq': _L0_attn_in['Wq'], 'L0_attn_bq': _L0_attn_in['bq'], 'L0_attn_Wk': _L0_attn_in['Wk'], 'L0_attn_bk': _L0_attn_in['bk'], 'L0_attn_Wv': _L0_attn_in['Wv'], 'L0_attn_bv': _L0_attn_in['bv'], 'L0_attn_Wa': _L0_attn_in['Wa'], 'L0_attn_ba': _L0_attn_in['ba'], 'L0_attn_Wb': _L0_attn_in['Wb'], 'L0_attn_bb': _L0_attn_in['bb'], 'L0_attn_conv_q': _L0_attn_in['conv_q'], 'L0_attn_conv_k': _L0_attn_in['conv_k'], 'L0_attn_conv_v': _L0_attn_in['conv_v'], 'L0_attn_Wo': _L0_attn_in['Wo'], 'L0_attn_bo': _L0_attn_in['bo'], 'L0_ffn_in_proj_w': _L0_ffn_in['in_proj_w'], 'L0_ffn_in_proj_b': _L0_ffn_in['in_proj_b'], 'L0_ffn_out_w': _L0_ffn_in['out_w'], 'L0_ffn_out_b': _L0_ffn_in['out_b'], 'L0_ffn_gate_w': _L0_ffn_in['gate_w'], 'L0_ffn_gate_b': _L0_ffn_in['gate_b'], 'L0_ffn_w1': _L0_ffn_in['w1'], 'L0_ffn_b1': _L0_ffn_in['b1'], 'L0_ffn_w2': _L0_ffn_in['w2'], 'L0_ffn_b2': _L0_ffn_in['b2'], 'L0_ffn_ln1_g': _L0_ffn_in['ln1_g'], 'L0_ffn_ln1_b': _L0_ffn_in['ln1_b'], 'L0_ffn_ln2_g': _L0_ffn_in['ln2_g'], 'L0_ffn_ln2_b': _L0_ffn_in['ln2_b']}
    _x0 = _d['L0_attn_x']
    _d['L0_attn_x'] = jax.random.normal(jax.random.fold_in(jax.random.key(seed), 1), (4, 1024, 128), dtype=_x0.dtype)
    del _x0
    return _d

def reference(L0_attn_x, L0_attn_Wq, L0_attn_bq, L0_attn_Wk, L0_attn_bk, L0_attn_Wv, L0_attn_bv, L0_attn_Wa, L0_attn_ba, L0_attn_Wb, L0_attn_bb, L0_attn_conv_q, L0_attn_conv_k, L0_attn_conv_v, L0_attn_Wo, L0_attn_bo, L0_ffn_in_proj_w, L0_ffn_in_proj_b, L0_ffn_out_w, L0_ffn_out_b, L0_ffn_gate_w, L0_ffn_gate_b, L0_ffn_w1, L0_ffn_b1, L0_ffn_w2, L0_ffn_b2, L0_ffn_ln1_g, L0_ffn_ln1_b, L0_ffn_ln2_g, L0_ffn_ln2_b):

    def _L0_attn_ref(x, Wq, bq, Wk, bk, Wv, bv, Wa, ba, Wb, bb, conv_q, conv_k, conv_v, Wo, bo):
        import jax, jax.numpy as jnp
        import numpy as np
        DIM = 128
        H = 16
        DH = DIM // H
        K = 4
        B = 8
        N = 256
        EPS = 1e-06

        def _depthwise_conv_silu(x, w, n):
            pad = K // 2
            y = jax.lax.conv_general_dilated(x.transpose(0, 2, 1), w, window_strides=(1,), padding=[(pad, pad)], dimension_numbers=('NCH', 'OIH', 'NCH'), feature_group_count=x.shape[-1])
            y = y[..., :n]
            return jax.nn.silu(y).transpose(0, 2, 1)

        def _l2norm(x):
            return x / (jnp.linalg.norm(x, axis=-1, keepdims=True) + EPS)

        def _forward(x, Wq, bq, Wk, bk, Wv, bv, Wa, ba, Wb, bb, conv_q, conv_k, conv_v, Wo, bo):
            b_, n_, c_ = x.shape
            q = _l2norm(_depthwise_conv_silu(jax.nn.silu(x @ Wq.T + bq), conv_q, n_))
            k = _l2norm(_depthwise_conv_silu(jax.nn.silu(x @ Wk.T + bk), conv_k, n_))
            v = _depthwise_conv_silu(jax.nn.silu(x @ Wv.T + bv), conv_v, n_)
            a = jax.nn.sigmoid(x @ Wa.T + ba)
            bgate = jax.nn.sigmoid(x @ Wb.T + bb)
            q = q.reshape(b_, n_, H, DH).transpose(1, 0, 2, 3)
            k = k.reshape(b_, n_, H, DH).transpose(1, 0, 2, 3)
            v = v.reshape(b_, n_, H, DH).transpose(1, 0, 2, 3)
            a = a.transpose(1, 0, 2)
            bgate = bgate.transpose(1, 0, 2)
            S0 = jnp.zeros((b_, H, DH, DH), x.dtype)

            def step(S, inp):
                qt, kt, vt, at, bt = inp
                at = at[..., None, None]
                bt = bt[..., None, None]
                Sk = jnp.einsum('bhde,bhe->bhd', S, kt)
                outer_Sk_k = Sk[..., :, None] * kt[..., None, :]
                outer_v_k = vt[..., :, None] * kt[..., None, :]
                S_new = at * S - at * bt * outer_Sk_k + bt * outer_v_k
                ot = jnp.einsum('bhd,bhde->bhe', qt, S_new)
                return (S_new, ot)
            _, O = jax.lax.scan(step, S0, (q, k, v, a, bgate))
            O = O.transpose(1, 0, 2, 3).reshape(b_, n_, c_)
            return O @ Wo.T + bo
        return _forward(x, Wq, bq, Wk, bk, Wv, bv, Wa, ba, Wb, bb, conv_q, conv_k, conv_v, Wo, bo)

    def _L0_ffn_ref(src, in_proj_w, in_proj_b, out_w, out_b, gate_w, gate_b, w1, b1, w2, b2, ln1_g, ln1_b, ln2_g, ln2_b):
        import jax, jax.numpy as jnp
        import numpy as np
        S, B, D, H, E, K, F = (128, 4, 128, 16, 8, 2, 512)

        def _ln(x, g, b, eps=1e-05):
            mu = jnp.mean(x, axis=-1, keepdims=True)
            var = jnp.mean((x - mu) ** 2, axis=-1, keepdims=True)
            return (x - mu) * jax.lax.rsqrt(var + eps) * g + b
        s_len, bsz, d = src.shape
        dh = d // H
        qkv = src @ in_proj_w.T + in_proj_b
        q, k, v = jnp.split(qkv, 3, axis=-1)
        q = q.reshape(s_len, bsz, H, dh)
        k = k.reshape(s_len, bsz, H, dh)
        v = v.reshape(s_len, bsz, H, dh)
        scale = dh ** (-0.5)
        scores = jnp.einsum('sbhd,tbhd->bhst', q, k) * scale
        attn = jax.nn.softmax(scores, axis=-1)
        ctx = jnp.einsum('bhst,tbhd->sbhd', attn, v).reshape(s_len, bsz, d)
        attn_out = ctx @ out_w.T + out_b
        x = _ln(src + attn_out, ln1_g, ln1_b)
        tok = x.reshape(-1, d)
        n_tok = tok.shape[0]
        logits = tok @ gate_w.T + gate_b
        probs = jax.nn.softmax(logits, axis=-1)
        topv, topi = jax.lax.top_k(probs, K)
        topv = topv / jnp.sum(topv, axis=-1, keepdims=True)
        combine = jnp.zeros_like(probs).at[jnp.arange(n_tok)[:, None], topi].set(topv)
        moe_out = jnp.zeros_like(tok)
        for e in range(E):
            h = jax.nn.relu(tok @ w1[e].T + b1[e]) @ w2[e].T + b2[e]
            moe_out = moe_out + combine[:, e:e + 1] * h
        moe_out = moe_out.reshape(s_len, bsz, d)
        return _ln(x + moe_out, ln2_g, ln2_b)
    x = L0_attn_x
    x = _layernorm(x + _L0_attn_ref(x, L0_attn_Wq, L0_attn_bq, L0_attn_Wk, L0_attn_bk, L0_attn_Wv, L0_attn_bv, L0_attn_Wa, L0_attn_ba, L0_attn_Wb, L0_attn_bb, L0_attn_conv_q, L0_attn_conv_k, L0_attn_conv_v, L0_attn_Wo, L0_attn_bo), axis=-1)
    x = _layernorm(x + _L0_ffn_ref(x, L0_ffn_in_proj_w, L0_ffn_in_proj_b, L0_ffn_out_w, L0_ffn_out_b, L0_ffn_gate_w, L0_ffn_gate_b, L0_ffn_w1, L0_ffn_b1, L0_ffn_w2, L0_ffn_b2, L0_ffn_ln1_g, L0_ffn_ln1_b, L0_ffn_ln2_g, L0_ffn_ln2_b), axis=-1)
    return x

_drawn_inputs = setup_inputs


def setup_inputs(seed=0):
    import zlib

    import numpy as np

    out = dict(_drawn_inputs(seed))
    spreads = {'L0_attn_bq': (0.0, 0.8),
     'L0_attn_bk': (0.0, 0.8),
     'L0_attn_bv': (0.0, 0.8),
     'L0_attn_ba': (0.0, 0.8),
     'L0_attn_bb': (0.0, 0.8),
     'L0_attn_bo': (0.0, 0.286),
     'L0_ffn_in_proj_b': (0.0, 0.559),
     'L0_ffn_out_b': (0.0, 0.1),
     'L0_ffn_gate_b': (0.0, 0.1),
     'L0_ffn_b1': (0.0, 0.789),
     'L0_ffn_b2': (0.0, 0.1),
     'L0_ffn_ln1_g': (1.0, 0.2),
     'L0_ffn_ln1_b': (0.0, 0.1),
     'L0_ffn_ln2_g': (1.0, 0.2),
     'L0_ffn_ln2_b': (0.0, 0.1)}
    factors = {'L0_attn_Wq': 8.0,
     'L0_attn_Wk': 8.0,
     'L0_attn_Wv': 8.0,
     'L0_attn_Wa': 8.0,
     'L0_attn_Wb': 8.0,
     'L0_attn_conv_q': 8.0,
     'L0_attn_conv_k': 8.0,
     'L0_attn_conv_v': 8.0,
     'L0_attn_Wo': 8.0,
     'L0_ffn_in_proj_w': 3.953,
     'L0_ffn_out_w': 2.996}
    for name, (base, spread) in spreads.items():
        noise = np.random.default_rng([zlib.crc32(name.encode()), seed]).standard_normal(out[name].shape)
        drawn = base * np.exp(spread * noise) if base else spread * noise
        out[name] = jnp.asarray(drawn.astype(out[name].dtype))
    for name, factor in factors.items():
        out[name] = (out[name] * factor).astype(out[name].dtype)
    return out
```

```python
import concourse.bass as bass
from concourse import mybir
from contextlib import ExitStack
import numpy as np

F32 = mybir.dt.float32
ALU = mybir.AluOpType
ACT = mybir.ActivationFunctionType
AX = mybir.AxisListType

B = 4
N = 1024
C = 128
H = 16
E = C // H
TAPS = 4
PAD = TAPS // 2
T = 128
NBLK = N // T
J = 4
CH = T // J
G = 4
DQ = E // 2
NE = 8
FF = 512
FT = FF // 128
L2_EPS = 1e-6
LN_EPS = 1e-5
SCALE = float(E) ** -0.5


class Queue:

    def __init__(self, name):
        self.name, self.items, self.count = name, [], 0

    def do(self, make, after=()):
        self.count += 1
        self.items.append((make, [m for m in after if m is not None], 1))
        return (self, self.count)

    def part(self, make, after=()):
        self.items.append((make, [m for m in after if m is not None], 0))

    def dma(self, make, sem, after=()):
        sem.count += 16
        self.items.append((make, [m for m in after if m is not None], sem))
        return (sem, sem.count)

    def wait(self, mark):
        self.items.append((None, [mark], 0))

    def emit(self, eng, sems):
        seen = {}
        for make, after, inc in self.items:
            for q, value in after:
                if seen.get(q.name, 0) < value:
                    eng.wait_ge(sems[q.name], value)
                    seen[q.name] = value
            if make is None:
                continue
            ins = make(eng)
            if inc == 1:
                ins.then_inc(sems[self.name], 1)
            elif inc:
                ins.then_inc(sems[inc.name], 16)


class DmaSem:
    def __init__(self, name):
        self.name, self.count = name, 0


class Banks:

    def __init__(self, aps):
        self.aps, self.freed, self.at = aps, [None] * len(aps), 0

    def take(self):
        i = self.at
        self.at = (i + 1) % len(self.aps)
        return i, self.aps[i], self.freed[i]


def interleave(lanes):
    lanes = [list(lane) for lane in lanes if lane]
    total = max((len(x) for x in lanes), default=0)
    order = sorted(((k + 0.5) / len(x), w, k) for w, x in enumerate(lanes) for k in range(len(x)))
    for _, w, k in order:
        lanes[w][k]()


def build(nc, io):
    ctx = ExitStack()

    def sb(name, shape):
        return ctx.enter_context(nc.sbuf_tensor(name, shape, F32))

    with ctx:
        pe, dve, act, pool, sp = (Queue(n) for n in ("pe", "dve", "act", "pool", "sp"))

        w_qkv = sb("w_qkv", [C, 3, C])
        b_qkv = sb("b_qkv", [C, 3])
        w_gates = sb("w_gates", [C, 2 * H])
        b_gates = sb("b_gates", [128, 2])
        w_conv = sb("w_conv", [C, 3, TAPS])
        w_o = sb("w_o", [C, C])
        b_rows = sb("b_rows", [1, 2, C])
        w_in = sb("w_in", [C, 3 * C])
        b_in = sb("b_in", [128, 3 * C])
        w_out = sb("w_out", [C, C])
        w_gate = sb("w_gate", [C, NE])
        b_gate = sb("b_gate", [128, NE])
        w1 = sb("w1", [C, NE, FF])
        b1 = sb("b1", [128, NE, FT])
        w2 = sb("w2", [128, NE, FT, C])
        b2 = sb("b2", [NE, C])
        ln_gb = sb("ln_gb", [128, 4, C])
        ident = sb("ident", [128, 128])
        fold = sb("fold", [128, B * H])
        tril = sb("tril", [128, NE, NE])
        ones = sb("ones", [1, 128])
        eps_ln = sb("eps_ln", [128, 1])

        NX = 3
        x_ch = [sb(f"x_ch{i}", [C, B, T]) for i in range(2)]
        x_tok = sb("x_tok", [T, B, C])
        proj = [sb(f"proj{i}", [C, 3, B, T + TAPS - 1]) for i in range(2)]
        conv_acc = sb("conv_acc", [C, B, T])
        conv_out = [sb(f"conv_out{i}", [C, B, T]) for i in range(2)]
        gates_tok = sb("gates_tok", [T, 2, B * H, 2])
        sq_junk = sb("sq_junk", [T, C])
        ssq = sb("ssq", [T, 2, B])
        q_tok = sb("q_tok", [T, B, C])
        v_tok = sb("v_tok", [T, B, C])
        k_tok = sb("k_tok", [T, B * H, 2, E])
        k_w = [sb(f"k_w{i}", [128, T, E]) for i in range(3)]
        v_w = [sb(f"v_w{i}", [128, T, DQ]) for i in range(2)]
        q_w = [sb(f"q_w{i}", [128, T, DQ]) for i in range(3)]
        ab_w = [sb(f"ab_w{i}", [128, 2, T]) for i in range(2)]
        decay = [sb(f"decay{i}", [128, T]) for i in range(2)]
        ratio = [sb(f"ratio{i}", [128, CH, 3, J]) for i in range(2)]
        bratio = sb("bratio", [128, CH, 3, J])
        kk_prod = sb("kk_prod", [128, CH, J - 1, E])
        lmat = sb("lmat", [128, CH, 3, J])
        bdecay = sb("bdecay", [128, T])
        solve = sb("solve", [128, CH, J, E + DQ])
        solve_t = sb("solve_t", [128, CH, E + DQ])
        kend = sb("kend", [128, CH, J, E])
        eend = sb("eend", [128, CH, J])
        sk_buf = sb("sk_buf", [128, 2, G, J * DQ, E + 1])
        uk_buf = sb("uk_buf", [128, DQ, E, J])
        uk_sum = sb("uk_sum", [128, DQ * E])
        u_neg = [sb(f"u_neg{i}", [128, CH, J, DQ]) for i in range(2)]
        state = [sb(f"state{i}", [128, CH, DQ, E]) for i in range(2)]
        read_prod = sb("read_prod", [128, CH, E, DQ])
        o_w = sb("o_w", [128, CH, J, E])
        uq = sb("uq", [128, CH, J])
        uq_prod = sb("uq_prod", [128, CH, J, DQ])
        o_tok = sb("o_tok", [T, B, C])
        ch_a = sb("ch_a", [C, B, T])
        ch_x = [sb(f"ch_x{i}", [C, B, T]) for i in range(2)]
        x1 = [sb(f"x1_{i}", [T, B, C]) for i in range(2)]
        x2 = [sb(f"x2_{i}", [T, B, C]) for i in range(2)]
        stats = sb("stats", [T, B, 6])
        mv = sb("mv", [T, B, 2])
        rstd = sb("rstd", [T, B])
        stats_m = sb("stats_m", [T, B, 6])
        mv_m = sb("mv_m", [T, B, 2])
        rstd_m = sb("rstd_m", [T, B])
        attn_in = sb("attn_in", [T, B, 3 * C])
        pair = sb("pair", [T, B * C])
        score = sb("score", [T, B, H, B])
        smax = sb("smax", [T, B, H])
        ctx_tok = sb("ctx_tok", [T, B, C])
        logit = sb("logit", [T, B, NE])
        lmax = sb("lmax", [T, B])
        lcmp = sb("lcmp", [T, B, NE, NE])
        lcmp2 = sb("lcmp2", [T, B, NE, NE])
        rank = sb("rank", [T, B, NE])
        combine = [sb(f"combine{i}", [T, B, NE]) for i in range(2)]
        combine_t = [sb(f"combine_t{i}", [NE, B, T]) for i in range(2)]
        hidden = sb("hidden", [128, 2 * FT, B * T])
        moe_acc = sb("moe_acc", [T, B, C])
        y_out = [sb(f"y_out{i}", [T, B, C]) for i in range(2)]

        ps = [ctx.enter_context(nc.psum_tensor(f"ps{i}", [128, 512], F32)) for i in range(8)]
        banks_a, banks_p, banks_h, banks_y = Banks(ps[0:2]), Banks(ps[2:4]), Banks(ps[4:6]), Banks(ps[6:8])

        s_const = DmaSem("s_const")
        s_x = [DmaSem(f"s_x{i}") for i in range(2)]
        s_xt = [DmaSem(f"s_xt{i}") for i in range(2)]
        s_y = [DmaSem(f"s_y{i}") for i in range(2)]

        def load(dst, name, shape=None):
            src = io[name]
            return sp.dma(lambda e: e.dma_start(dst, src), s_const)

        def load_x_ch(n, after=()):
            return sp.dma(lambda e: e.dma_start(x_ch[n % 2][:, :, :], io["x_ch"][:, n, :, :]), s_x[n % 2], after)

        x_ch_loaded = {0: load_x_ch(0)}
        load(w_qkv[:, :, :], "w_qkv")
        load(b_qkv[:, :], "b_qkv")
        load(w_gates[:, :], "w_gates")
        load(b_gates[:, :], "b_gates")
        load(w_conv[:, :, :], "w_conv")
        x_ch_loaded[1] = load_x_ch(1)
        load(w_o[:, :], "w_o")
        load(b_rows[:, :, :], "b_rows")
        load(w_in[:, :], "w_in")
        load(b_in[:, :], "b_in")
        load(w_out[:, :], "w_out")
        load(w_gate[:, :], "w_gate")
        load(b_gate[:, :], "b_gate")
        load(b1[:, :, :], "b1")
        load(b2[:, :], "b2")
        load(ln_gb[:, :, :], "ln_gb")
        load(fold[:, :], "fold")
        load(tril[:, :, :], "tril")
        load(ident[:, :], "ident")
        load(w1[:, :, :], "w1")
        consts = load(w2[:, :, :, :], "w2")

        const_small = consts
        ones_set = pool.do(lambda e: e.memset(ones[:, :], 1.0))
        eps_set = pool.do(lambda e: e.memset(eps_ln[:, :], LN_EPS))
        front_set = pool.do(lambda e: e.memset(proj[0][:, :, :, 0:PAD], 0.0))
        state_set = pool.do(lambda e: e.memset(state[0][:, 0, :, :], 0.0))

        m = {}

        def g(*key):
            return m.get(key)

        def project(n):
            def proj_one(k):
                def run():
                    i, bank, freed = banks_a.take()
                    mm = pe.do(lambda e: e.matmul(bank[:, :], w_qkv[:, k, :], x_ch[n % 2][:, :, :].rearrange("c b t -> c (b t)"),
                                                  start=True, stop=True),
                               [const_small, x_ch_loaded[n], freed])
                    here, there = proj[n % 2], proj[1 - n % 2]
                    banks_a.freed[i] = act.do(
                        lambda e: e.activation(here[:, k, :, PAD:PAD + T], bank[:, :].rearrange("c (b t) -> c b t", b=B), ACT.Silu, bias=b_qkv[:, k:k + 1]),
                        [mm, const_small, g("conv", n - 2, k)])
                    done = banks_a.freed[i]
                    if n:
                        done = act.do(lambda e: e.activation(there[:, k, :, PAD + T:], here[:, k, :, PAD:PAD + 1], ACT.Copy), [done])
                    m["proj", n, k] = done
                return run

            def gate_mm():
                i, bank, freed = banks_a.take()
                for b in range(B):
                    dst = bank[:, 0:2 * B * H].rearrange("t (k b h) -> t b k h", k=2, b=B)[:, b, :, :]
                    mk = (pe.do if b == B - 1 else pe.part)(
                        lambda e, b=b, dst=dst: e.matmul(dst, x_ch[n % 2][:, b, :], w_gates[:, :].rearrange("c (k h) -> c k h", k=2),
                                                         start=True, stop=True),
                        [const_small, x_ch_loaded[n], freed])
                ev = dve.do(lambda e, bank=bank: e.tensor_copy(
                    gates_tok[:, :, :, :],
                    bank[:, 0:2 * B * H].rearrange("t (k g) -> t k g", k=2).unsqueeze(3).to_broadcast([T, 2, B * H, 2])), [mk, g("gate_t", n - 1)])
                banks_a.freed[i] = ev
                m["x_ch_read", n] = mk
                if n + 2 < NBLK:
                    x_ch_loaded[n + 2] = load_x_ch(n + 2, [mk])
                i, bank, freed = banks_a.take()
                pe.part(lambda e: e.transpose(bank[:, 0:T], gates_tok[:, 0, :, :].rearrange("t g d -> t (g d)"), ident[:, :]), [ev, freed])
                tr = pe.do(lambda e: e.transpose(bank[:, T:2 * T], gates_tok[:, 1, :, :].rearrange("t g d -> t (g d)"), ident[:, :]))
                m["gate_t", n] = tr
                for k in range(2):
                    banks_a.freed[i] = act.do(
                        lambda e, k=k: e.activation(ab_w[n % 2][:, k, :], bank[:, k * T:(k + 1) * T], ACT.Sigmoid, bias=b_gates[:, k:k + 1]),
                        [tr, g("prep_done", n - 2)])
                m["ab", n] = banks_a.freed[i]
            return [proj_one(0), proj_one(1), proj_one(2), gate_mm]

        def conv_norm(n):
            ahead = min(n + 1, NBLK - 1)
            steps = []

            def conv_one(k):
                def run():
                    done, back = g("proj", ahead, k), None
                    here, there = proj[n % 2], proj[1 - n % 2]
                    src = [here[:, k, :, j:j + T] for j in range(TAPS)]
                    if n + 1 == NBLK:
                        back = pool.do(lambda e: e.memset(here[:, k, :, PAD + T:], 0.0), [done, g("conv", n - 2, k)])
                    a = dve.do(lambda e: e.tensor_scalar(conv_acc[:, :, :], src[0], w_conv[:, k, 0:1], None, ALU.mult),
                               [done, front_set, const_small, g("conv_silu"), g("front", n, k), back])
                    for j in range(1, TAPS):
                        a = dve.do(lambda e, j=j: e.scalar_tensor_tensor(conv_acc[:, :, :], src[j], w_conv[:, k, j:j + 1],
                                                                         conv_acc[:, :, :], ALU.mult, ALU.add), [a])
                    m["conv", n, k] = a
                    if n + 1 < NBLK:
                        m["front", n + 1, k] = act.do(lambda e: e.activation(there[:, k, :, 0:PAD], here[:, k, :, T:T + PAD], ACT.Copy), [a])
                    dst = conv_out[k % 2]
                    s = act.do(lambda e: e.activation(dst[:, :, :], conv_acc[:, :, :], ACT.Silu), [a, g("conv_out_read", k % 2)])
                    m["conv_silu",] = s
                    i, bank, freed = banks_a.take()
                    for b in range(B):
                        tr = (pe.do if b == B - 1 else pe.part)(
                            lambda e, b=b: e.transpose(bank[:, b * C:(b + 1) * C], dst[:, b, :], ident[:, :]), [s, freed])
                    m["conv_out_read", k % 2] = tr
                    if k == 2:
                        banks_a.freed[i] = act.do(lambda e: e.activation(v_tok[:, :, :].rearrange("t b c -> t (b c)"), bank[:, :], ACT.Copy),
                                                  [tr, g("v_tok_read")])
                        m["v_tok", n] = banks_a.freed[i]
                    else:
                        for b in range(B):
                            sq = act.do(lambda e, b=b: e.activation(sq_junk[:, :], bank[:, b * C:(b + 1) * C], ACT.Square,
                                                                    accum_out=ssq[:, k, b:b + 1]), [tr, g("ssq_read", k), g("sq_prev")])
                            m["sq_prev",] = sq
                        nrm = act.do(lambda e: e.activation(ssq[:, k, :], ssq[:, k, :], ACT.Sqrt), [sq])
                        ad = dve.do(lambda e: e.tensor_scalar(ssq[:, k, :], ssq[:, k, :], L2_EPS, None, ALU.add), [nrm])
                        rc = dve.do(lambda e: e.reciprocal(ssq[:, k, :], ssq[:, k, :]), [ad])
                        out = k_tok[:, :, 0, :].rearrange("t (b h) e -> t b h e", b=B) if k else q_tok[:, :, :].rearrange("t b (h e) -> t b h e", e=E)
                        banks_a.freed[i] = dve.do(lambda e: e.tensor_tensor(
                            out, bank[:, :].rearrange("t (b h e) -> t b h e", b=B, e=E),
                            ssq[:, k, :].unsqueeze(2).unsqueeze(3).to_broadcast([T, B, H, E]), ALU.mult),
                            [rc, tr, g(("q_tok_read", "k_tok_read")[k])])
                        m["ssq_read", k] = banks_a.freed[i]
                        m[("q_tok", "k_tok")[k], n] = banks_a.freed[i]
                        if k:
                            m["k_tok", n] = pool.do(lambda e: e.tensor_copy(k_tok[:, :, 1, :], k_tok[:, :, 0, :]), [banks_a.freed[i]])
                return run

            def to_state(k):
                def run():
                    tok = (q_tok, None, v_tok)[k]
                    name = ("q", "k", "v")[k]
                    dst, old = ((q_w[n % 3], g("o_done", n - 3)), (k_w[n % 3], g("o_done", n - 3)), (v_w[n % 2], g("prep_done", n - 2)))[k]
                    for half in range(2 if k == 1 else 1):
                        i, bank, freed = banks_a.take()
                        for d in range(4):
                            if k == 1:
                                src = k_tok[:, :, :, :].rearrange("t g s e -> t (g s) e")[:, :, 4 * half + d]
                            else:
                                src = tok[:, :, :].rearrange("t b (g d) -> t (b g) d", d=DQ)[:, :, d]
                            tr = (pe.do if d == 3 else pe.part)(
                                lambda e, d=d, src=src, bank=bank: e.transpose(bank[:, d * T:(d + 1) * T], src, ident[:, :]),
                                [g(name + "_tok", n), freed])
                        out = dst[:, :, 4 * half:4 * half + 4].rearrange("p t d -> p d t") if k == 1 else dst[:, :, :].rearrange("p t d -> p d t")
                        banks_a.freed[i] = act.do(lambda e, out=out, bank=bank: e.activation(
                            out, bank[:, :].rearrange("p (d t) -> p d t", d=4), ACT.Copy), [tr, old])
                    m[name + "_w", n] = banks_a.freed[i]
                    m[name + "_tok_read",] = tr
                return run
            return [conv_one(0), to_state(0), conv_one(1), to_state(1), conv_one(2), to_state(2)]

        def chunked(ap):
            return ap.rearrange("p (c j) -> p c j", j=J)

        def prepare(n):
            p2, p3 = n % 2, n % 3

            def decays():
                a, b = chunked(ab_w[p2][:, 0, :]), chunked(ab_w[p2][:, 1, :])
                dec = chunked(decay[p2][:, :])
                rat = ratio[p2]
                x = dve.do(lambda e: e.tensor_copy(dec[:, :, 0], a[:, :, 0]), [g("ab", n)])
                for j in range(1, J):
                    x = dve.do(lambda e, j=j: e.tensor_tensor(dec[:, :, j], dec[:, :, j - 1], a[:, :, j], ALU.mult), [x])
                y = dve.do(lambda e: e.tensor_copy(rat[:, :, 0, 1:J], a[:, :, 1:J]))
                for lag in range(2, J):
                    y = dve.do(lambda e, lag=lag: e.tensor_tensor(rat[:, :, lag - 1, lag:J], rat[:, :, lag - 2, lag:J],
                                                                  a[:, :, 1:J - lag + 1], ALU.mult), [y])
                z = x
                for lag in range(1, J):
                    z = dve.do(lambda e, lag=lag: e.tensor_tensor(bratio[:, :, lag - 1, lag:J], rat[:, :, lag - 1, lag:J],
                                                                  b[:, :, lag:J], ALU.mult), [y])
                w = dve.do(lambda e: e.tensor_tensor(bdecay[:, :], decay[p2][:, :], ab_w[p2][:, 1, :], ALU.mult), [x])
                s = dve.do(lambda e: e.memset(eend[:, :, J - 1], -1.0))
                for lag in range(1, J):
                    s = dve.do(lambda e, lag=lag: e.tensor_scalar(eend[:, :, J - 1 - lag], rat[:, :, lag - 1, J - 1], -1.0, None, ALU.mult), [y])
                m["decays", n], m["bratio", n], m["bdecay", n] = s, z, w

            def rhs():
                k, v = k_w[p3], v_w[p2]
                kc = k[:, :, :].rearrange("p (c j) e -> p c j e", j=J)
                r1 = dve.do(lambda e: e.tensor_tensor(solve[:, :, :, 0:E].rearrange("p c j e -> p (c j) e"), k[:, :, :],
                                                      bdecay[:, :].unsqueeze(2).to_broadcast([128, T, E]), ALU.mult), [g("bdecay", n), g("k_w", n)])
                r2 = dve.do(lambda e: e.tensor_tensor(solve[:, :, :, E:].rearrange("p c j d -> p (c j) d"), v[:, :, :],
                                                      ab_w[p2][:, 1, :].unsqueeze(2).to_broadcast([128, T, DQ]), ALU.mult), [g("ab", n), g("v_w", n)])
                r3 = dve.do(lambda e: e.tensor_tensor(kend[:, :, :, :].rearrange("p c j e -> p (c j) e"), k[:, :, :],
                                                      eend[:, :, :].rearrange("p c j -> p (c j)").unsqueeze(2).to_broadcast([128, T, E]), ALU.mult),
                            [g("decays", n)])
                m["rhs", n], m["kend", n] = r2, r3

            def dots(lag):
                def run():
                    kc = k_w[p3][:, :, :].rearrange("p (c j) e -> p c j e", j=J)
                    x = dve.do(lambda e: e.tensor_tensor(kk_prod[:, :, 0:J - lag, :], kc[:, :, lag:J, :], kc[:, :, 0:J - lag, :], ALU.mult),
                               [g("k_w", n), g("kk_read")])
                    x = dve.do(lambda e: e.tensor_reduce(lmat[:, :, lag - 1, lag:J], kk_prod[:, :, 0:J - lag, :], AX.X, ALU.add), [x])
                    m["kk_read",] = x
                    m["lmat", n] = dve.do(lambda e: e.tensor_tensor(lmat[:, :, lag - 1, lag:J], lmat[:, :, lag - 1, lag:J],
                                                                    bratio[:, :, lag - 1, lag:J], ALU.mult), [x, g("bratio", n)])
                return run

            def substitute(j, i):
                def run():
                    x = dve.do(lambda e: e.tensor_tensor(solve_t[:, :, :], solve[:, :, i, :],
                                                         lmat[:, :, j - i - 1, j].unsqueeze(2).to_broadcast([128, CH, E + DQ]), ALU.mult),
                               [g("lmat", n), g("rhs", n), g("sub")])
                    m["sub",] = dve.do(lambda e: e.tensor_tensor(solve[:, :, j, :], solve[:, :, j, :], solve_t[:, :, :], ALU.subtract), [x])
                return run

            def lay_u0():
                m["prep", n] = m["prep_done", n] = g("sub")
            return [decays, rhs] + [dots(lag) for lag in range(1, J)] + \
                [substitute(j, i) for j in range(1, J) for i in range(j)] + [lay_u0]

        def chunks(n):
            p2 = n % 2

            def lay_u0(q):
                m["laid", n, q] = act.do(lambda e: e.activation(
                    sk_buf[:, q % 2, :, :, E].rearrange("p c (j d) -> p c j d", j=J), solve[:, G * q:G * (q + 1), :, E:], ACT.Copy, scale=-1.0),
                    [g("prep", n), g("laid_read", q % 2)])

            def one(c):
                def run():
                    if c == 0:
                        lay_u0(0)
                    if c % G == 0 and c + G < CH:
                        lay_u0(c // G + 1)
                    s_in = state[p2][:, c, :, :]
                    s_out = state[p2][:, c + 1, :, :] if c + 1 < CH else state[1 - p2][:, 0, :, :]
                    w = solve[:, c, :, 0:E]
                    sk = sk_buf[:, c // G % 2, c % G, :, :]
                    un = u_neg[p2][:, c, :, :]
                    x = dve.do(lambda e: e.tensor_tensor(
                        sk[:, :, 0:E].rearrange("p (j d) e -> p j d e", j=J), s_in.unsqueeze(1).to_broadcast([128, J, DQ, E]),
                        w.unsqueeze(2).to_broadcast([128, J, DQ, E]), ALU.mult), [state_set, g("state"), g("prep", n)])
                    x = dve.do(lambda e: e.tensor_reduce(un.rearrange("p j d -> p (j d)"), sk, AX.X, ALU.add), [x, g("laid", n, c // G), g("o_done", n - 2)])
                    m["laid_read", c // G % 2] = x
                    x = dve.do(lambda e: e.tensor_tensor(
                        uk_buf[:, :, :, :], un.rearrange("p j d -> p d j").unsqueeze(2).to_broadcast([128, DQ, E, J]),
                        kend[:, c, :, :].rearrange("p j e -> p e j").unsqueeze(1).to_broadcast([128, DQ, E, J]), ALU.mult), [x])
                    x = dve.do(lambda e: e.tensor_reduce(uk_sum[:, :], uk_buf[:, :, :, :].rearrange("p d e j -> p (d e) j"), AX.X, ALU.add), [x])
                    m["state",] = dve.do(lambda e: e.scalar_tensor_tensor(
                        s_out.rearrange("p d e -> p (d e)"), s_in.rearrange("p d e -> p (d e)"),
                        decay[p2][:, c * J + J - 1:c * J + J], uk_sum[:, :], ALU.mult, ALU.add), [x, g("o_done", n - 1) if c + 1 == CH else None])
                    if c + 1 == CH:
                        m["chunks", n] = m["state",]
                return run
            return [one(c) for c in range(CH)]

        def read_out(n):
            p2, p3 = n % 2, n % 3
            qc = q_w[p3][:, :, :].rearrange("p (c j) d -> p c j d", j=J)
            kc = k_w[p3][:, :, :].rearrange("p (c j) e -> p c j e", j=J)

            def from_state(j):
                def run():
                    x = dve.do(lambda e: e.tensor_tensor(
                        read_prod[:, :, :, :], state[p2][:, :, :, :].rearrange("p c d e -> p c e d"),
                        qc[:, :, j, :].unsqueeze(2).to_broadcast([128, CH, E, DQ]), ALU.mult), [g("chunks", n), g("q_w", n), g("read_red")])
                    m["read_red",] = dve.do(lambda e: e.tensor_reduce(o_w[:, :, j, :], read_prod[:, :, :, :], AX.X, ALU.add), [x, g("o_w_read")])
                return run

            def scale():
                m["o_w",] = dve.do(lambda e: e.tensor_tensor(
                    o_w[:, :, :, :].rearrange("p c j e -> p (c j) e"), o_w[:, :, :, :].rearrange("p c j e -> p (c j) e"),
                    decay[p2][:, :].unsqueeze(2).to_broadcast([128, T, E]), ALU.mult), [g("read_red")])

            def lag_part(lag):
                def run():
                    w = J - lag
                    x = dve.do(lambda e: e.tensor_tensor(uq_prod[:, :, 0:w, :], qc[:, :, lag:J, :], u_neg[p2][:, :, 0:w, :], ALU.mult), [g("uq")])
                    x = dve.do(lambda e: e.tensor_reduce(uq[:, :, 0:w], uq_prod[:, :, 0:w, :], AX.X, ALU.add), [x, g("ow")])
                    if lag:
                        x = dve.do(lambda e: e.tensor_tensor(uq[:, :, 0:w], uq[:, :, 0:w], ratio[p2][:, :, lag - 1, lag:J], ALU.mult), [x])
                    m["uq",] = x
                    m["ow",] = dve.do(lambda e: e.tensor_tensor(read_prod[:, :, :, :].rearrange("p c e d -> p c (e d)").rearrange("p c (j e) -> p c j e", j=J)[:, :, 0:w, :], kc[:, :, 0:w, :],
                                                                uq[:, :, 0:w].unsqueeze(3).to_broadcast([128, CH, w, E]), ALU.mult), [x, g("o_w")])
                    m["o_w",] = dve.do(lambda e: e.tensor_tensor(o_w[:, :, lag:J, :], o_w[:, :, lag:J, :], read_prod[:, :, :, :].rearrange("p c e d -> p c (e d)").rearrange("p c (j e) -> p c j e", j=J)[:, :, 0:w, :], ALU.subtract),
                                       [g("ow"), g("o_w")])
                    if lag == J - 1:
                        m["o_done", n] = m["o_w",]
                return run
            return [from_state(j) for j in range(J)] + [scale] + [lag_part(lag) for lag in range(J)]

        def transpose4(banks, src, dst, after, old):
            i, bank, freed = banks.take()
            for b in range(B):
                tr = (pe.do if b == B - 1 else pe.part)(
                    lambda e, b=b: e.transpose(bank[:, b * 128:(b + 1) * 128], src[:, b, :], ident[:, :]), [after, freed, const_small])
            banks.freed[i] = act.do(lambda e: e.activation(dst.rearrange("c b t -> c (b t)"), bank[:, :], ACT.Copy), [tr, old])
            return tr, banks.freed[i]

        def dense(banks, src, w, bias_row, after):
            i, bank, freed = banks.take()
            for b in range(B):
                pe.part(lambda e, b=b: e.matmul(bank[:, b * C:(b + 1) * C], src[:, b, :], w, start=True, stop=False), [after, freed, const_small])
                mm = (pe.do if b == B - 1 else pe.part)(
                    lambda e, b=b: e.matmul(bank[:, b * C:(b + 1) * C], ones[:, :], bias_row, start=False, stop=True), [ones_set])
            return i, bank, mm

        def layer_norm(src, dst, st, mvt, rs, after, old, gb=None):
            for b in range(B):
                x = dve.do(lambda e, b=b: e.bn_stats(st[:, b, :], src[:, b, :]), [after])
            for b in range(B):
                y = dve.do(lambda e, b=b: e.bn_aggr(mvt[:, b, :], st[:, b, :]), [x])
            s = act.do(lambda e: e.activation(rs[:, :], mvt[:, :, 1], ACT.Sqrt, bias=eps_ln[:, 0:1]), [y, eps_set])
            r = dve.do(lambda e: e.reciprocal(rs[:, :], rs[:, :]), [s])
            for b in range(B):
                z = dve.do(lambda e, b=b: e.tensor_scalar(dst[:, b, :], src[:, b, :], mvt[:, b, 0:1], rs[:, b:b + 1], ALU.subtract, ALU.mult), [r, old])
            if gb is not None:
                for k, op in ((0, ALU.mult), (1, ALU.add)):
                    z = dve.do(lambda e, k=k, op=op: e.tensor_tensor(dst, dst, ln_gb[:, gb + k, :].unsqueeze(1).to_broadcast([T, B, C]), op),
                               [z, const_small])
            return z

        def mixer_out(n):
            p2 = n % 2

            def load_tok():
                m["x_tok", n] = sp.dma(lambda e: e.dma_start(x_tok[:, :, :], io["x"][:, n * T:(n + 1) * T, :].rearrange("b t c -> t b c")),
                                       s_xt[p2], [g("x_tok_read", n - 1)])

            def fold_halves():
                i, bank, freed = banks_p.take()
                ow = o_w[:, :, :, :].rearrange("p c j e -> p (c j) e")
                out = bank[:, :].rearrange("t (g e) -> t g e", e=E)
                for x in range(E):
                    mm = (pe.do if x == E - 1 else pe.part)(
                        lambda e, x=x: e.matmul(out[:, :, x], ow[:, :, x], fold[:, :], start=True, stop=True), [g("o_done", n), freed, const_small])
                m["o_w_read",] = mm
                banks_p.freed[i] = act.do(lambda e: e.activation(o_tok[:, :, :].rearrange("t b c -> t (b c)"), bank[:, :], ACT.Copy), [mm, g("o_tok_read")])
                m["o_tok",] = banks_p.freed[i]

            def to_ch():
                m["o_tok_read",], m["ch_a",] = transpose4(banks_p, o_tok, ch_a[:, :, :], g("o_tok"), g("ch_a_read"))

            def out_proj():
                i, bank, mm = dense(banks_p, ch_a, w_o[:, :], b_rows[:, 0, :], g("ch_a"))
                m["ch_a_read",] = mm
                banks_p.freed[i] = dve.do(lambda e: e.tensor_tensor(x1[p2][:, :, :], bank[:, :].rearrange("t (b c) -> t b c", b=B), x_tok[:, :, :], ALU.add),
                                          [mm, g("x_tok", n), g("final", n - 2)])
                m["x_tok_read", n] = banks_p.freed[i]
                m["x1", n] = layer_norm(x1[p2], x1[p2][:, :, :], stats, mv, rstd, banks_p.freed[i], None)

            def x1_ch():
                _, m["x1_ch",] = transpose4(banks_p, x1[p2], ch_a[:, :, :], g("x1", n), g("ch_a_read"))
            return [load_tok, fold_halves, to_ch, out_proj, x1_ch]

        def attention(n):
            p2 = n % 2

            def in_proj(b):
                def run():
                    i, bank, freed = banks_p.take()
                    mm = pe.do(lambda e: e.matmul(bank[:, 0:3 * C], ch_a[:, b, :], w_in[:, :], start=True, stop=True), [g("x1_ch"), freed])
                    banks_p.freed[i] = dve.do(lambda e: e.tensor_tensor(attn_in[:, b, :], bank[:, 0:3 * C], b_in[:, :], ALU.add), [mm])
                    m["ch_a_read",] = mm
                    m["attn_in",] = banks_p.freed[i]
                return run

            def scores(s):
                def run():
                    x = dve.do(lambda e: e.tensor_tensor(pair[:, :].rearrange("t (u c) -> t u c", u=B),
                                                         attn_in[:, s, 0:C].unsqueeze(1).to_broadcast([T, B, C]), attn_in[:, :, C:2 * C], ALU.mult),
                               [g("attn_in"), g("pair")])
                    m["pair",] = dve.do(lambda e: e.tensor_reduce(score[:, s, :, :].rearrange("t h u -> t u h"),
                                                                  pair[:, :].rearrange("t (u h e) -> t u h e", u=B, e=E), AX.X, ALU.add), [x, g("ctx")])
                return run

            def softmax():
                sc = score[:, :, :, :].rearrange("t s h u -> t (s h) u")
                mx = smax[:, :, :].rearrange("t s h -> t (s h)")
                bc = mx.unsqueeze(2).to_broadcast([T, B * H, B])
                x = dve.do(lambda e: e.tensor_reduce(mx, sc, AX.X, ALU.max), [g("pair")])
                x = dve.do(lambda e: e.tensor_tensor(sc, sc, bc, ALU.subtract), [x])
                x = act.do(lambda e: e.activation(sc, sc, ACT.Exp, scale=SCALE), [x])
                x = dve.do(lambda e: e.tensor_reduce(mx, sc, AX.X, ALU.add), [x])
                x = dve.do(lambda e: e.reciprocal(mx, mx), [x])
                m["attn",] = dve.do(lambda e: e.tensor_tensor(sc, sc, bc, ALU.mult), [x])

            def context(s):
                def run():
                    x = dve.do(lambda e: e.tensor_tensor(
                        pair[:, :].rearrange("t (u h e) -> t u h e", u=B, e=E),
                        score[:, s, :, :].rearrange("t h u -> t u h").unsqueeze(3).to_broadcast([T, B, H, E]),
                        attn_in[:, :, 2 * C:3 * C].rearrange("t u (h e) -> t u h e", e=E), ALU.mult), [g("attn"), g("pair")])
                    m["pair",] = m["ctx",] = dve.do(lambda e: e.tensor_reduce(ctx_tok[:, s, :], pair[:, :].rearrange("t (u c) -> t c u", u=B), AX.X, ALU.add),
                                                    [x, g("ctx_read")])
                return run

            def out_proj():
                m["ctx_read",], m["ch_a",] = transpose4(banks_p, ctx_tok, ch_a[:, :, :], g("ctx"), g("ch_a_read"))
                i, bank, mm = dense(banks_p, ch_a, w_out[:, :], b_rows[:, 1, :], g("ch_a"))
                m["ch_a_read",] = mm
                banks_p.freed[i] = dve.do(lambda e: e.tensor_tensor(x2[p2][:, :, :], bank[:, :].rearrange("t (b c) -> t b c", b=B), x1[p2][:, :, :], ALU.add),
                                          [mm, g("acc0", n - 2), g("x2_ch", n - 2)])
                m["x2", n] = layer_norm(x2[p2], x2[p2][:, :, :], stats, mv, rstd, banks_p.freed[i], None, gb=0)
            return [in_proj(b) for b in range(B)] + [scores(s) for s in range(B)] + [softmax] + [context(s) for s in range(B)] + [out_proj]

        def gate(n):
            p2 = n % 2

            def logits():
                _, m["x2_ch", n] = transpose4(banks_p, x2[p2], ch_x[p2][:, :, :], g("x2", n), g("moe_up", n - 2))
                i, bank, freed = banks_p.take()
                for b in range(B):
                    mm = (pe.do if b == B - 1 else pe.part)(
                        lambda e, b=b: e.matmul(bank[:, b * NE:(b + 1) * NE], ch_x[p2][:, b, :], w_gate[:, :], start=True, stop=True), [g("x2_ch", n), freed])
                banks_p.freed[i] = dve.do(lambda e: e.tensor_tensor(logit[:, :, :], bank[:, 0:B * NE].rearrange("t (b x) -> t b x", b=B),
                                                                    b_gate[:, :].unsqueeze(1).to_broadcast([T, B, NE]), ALU.add), [mm])
                m["logit",] = banks_p.freed[i]

            def select():
                bc = lmax[:, :].unsqueeze(2).to_broadcast([T, B, NE])
                lg = logit[:, :, :]
                x = dve.do(lambda e: e.tensor_reduce(lmax[:, :], lg, AX.X, ALU.max), [g("logit")])
                x = dve.do(lambda e: e.tensor_tensor(lg, lg, bc, ALU.subtract), [x])
                x = act.do(lambda e: e.activation(lg, lg, ACT.Exp), [x])
                x = dve.do(lambda e: e.tensor_reduce(lmax[:, :], lg, AX.X, ALU.add), [x])
                x = dve.do(lambda e: e.reciprocal(lmax[:, :], lmax[:, :]), [x])
                p = dve.do(lambda e: e.tensor_tensor(lg, lg, bc, ALU.mult), [x])
                for b in range(B):
                    pj = logit[:, b, :].unsqueeze(1).to_broadcast([T, NE, NE])
                    pi = logit[:, b, :].unsqueeze(2).to_broadcast([T, NE, NE])
                    dve.do(lambda e, b=b, pj=pj, pi=pi: e.tensor_tensor(lcmp[:, b, :, :], pj, pi, ALU.is_gt), [p])
                    x = dve.do(lambda e, b=b, pj=pj, pi=pi: e.tensor_tensor(lcmp2[:, b, :, :], pj, pi, ALU.is_equal), [p])
                x = dve.do(lambda e: e.tensor_tensor(lcmp2[:, :, :, :].rearrange("t b i j -> t b (i j)"), lcmp2[:, :, :, :].rearrange("t b i j -> t b (i j)"),
                                                     tril[:, :, :].rearrange("t i j -> t (i j)").unsqueeze(1).to_broadcast([T, B, NE * NE]), ALU.mult), [x])
                x = dve.do(lambda e: e.tensor_tensor(lcmp[:, :, :, :], lcmp[:, :, :, :], lcmp2[:, :, :, :], ALU.add), [x])
                x = dve.do(lambda e: e.tensor_reduce(rank[:, :, :].rearrange("t b i -> t (b i)"), lcmp[:, :, :, :].rearrange("t b i j -> t (b i) j"), AX.X, ALU.add), [x])
                x = dve.do(lambda e: e.scalar_tensor_tensor(lg, rank[:, :, :], 1.5, lg, ALU.is_lt, ALU.mult), [x])
                x = dve.do(lambda e: e.tensor_reduce(lmax[:, :], lg, AX.X, ALU.add), [x])
                x = dve.do(lambda e: e.reciprocal(lmax[:, :], lmax[:, :]), [x])
                m["combine", n] = dve.do(lambda e: e.tensor_tensor(combine[p2][:, :, :], lg, bc, ALU.mult), [x, g("moe", n - 2)])

            def combine_ch():
                i, bank, freed = banks_p.take()
                for b in range(B):
                    tr = (pe.do if b == B - 1 else pe.part)(
                        lambda e, b=b: e.transpose(bank[0:NE, b * T:(b + 1) * T], combine[p2][:, b, :], ident[:, :]), [g("combine", n), freed])
                banks_p.freed[i] = act.do(lambda e: e.activation(combine_t[p2][:, :, :].rearrange("x b t -> x (b t)"), bank[0:NE, :], ACT.Copy),
                                          [tr, g("acc0", n - 2)])
                m["combine_t", n] = banks_p.freed[i]
            return [logits, select, combine_ch]

        def experts(n):
            p2 = n % 2

            def start():
                i, bank, freed = banks_y.take()
                for b in range(B):
                    mm = (pe.do if b == B - 1 else pe.part)(
                        lambda e, b=b: e.matmul(bank[:, b * C:(b + 1) * C], combine_t[p2][:, b, :], b2[:, :], start=True, stop=True),
                        [g("combine_t", n), freed])
                banks_y.freed[i] = dve.do(lambda e: e.tensor_tensor(moe_acc[:, :, :], bank[:, :].rearrange("t (b c) -> t b c", b=B), x2[p2][:, :, :], ALU.add),
                                          [mm, g("x2", n)])
                m["acc0", n] = m["acc",] = banks_y.freed[i]

            def up(x, f):
                def run():
                    i, bank, freed = banks_h.take()
                    mm = pe.do(lambda e: e.matmul(bank[:, :], w1[:, x, f * 128:(f + 1) * 128], ch_x[p2][:, :, :].rearrange("c b t -> c (b t)"),
                                                  start=True, stop=True), [g("x2_ch", n), freed])
                    slot = (x % 2) * FT + f
                    banks_h.freed[i] = act.do(lambda e: e.activation(hidden[:, slot, :], bank[:, :], ACT.Relu, bias=b1[:, x, f:f + 1]),
                                              [mm, g("down", x % 2)])
                    m["hidden", slot] = banks_h.freed[i]
                    if x == NE - 1 and f == FT - 1:
                        m["moe_up", n] = mm
                return run

            def down(x):
                def run():
                    i, bank, freed = banks_y.take()
                    for b in range(B):
                        for f in range(FT):
                            slot = (x % 2) * FT + f
                            mm = (pe.do if b == B - 1 and f == FT - 1 else pe.part)(
                                lambda e, b=b, f=f, slot=slot: e.matmul(bank[:, b * C:(b + 1) * C], hidden[:, slot, b * T:(b + 1) * T], w2[:, x, f, :],
                                                                        start=f == 0, stop=f == FT - 1), [g("hidden", slot), freed])
                    m["down", x % 2] = mm
                    for b in range(B):
                        ac = dve.do(lambda e, b=b: e.scalar_tensor_tensor(moe_acc[:, b, :], bank[:, b * C:(b + 1) * C], combine[p2][:, b, x:x + 1],
                                                                          moe_acc[:, b, :], ALU.mult, ALU.add), [mm, g("acc")])
                    banks_y.freed[i] = ac
                    m["acc",] = ac
                    if x == NE - 1:
                        m["moe", n] = ac
                return run

            def finish():
                y = layer_norm(moe_acc, moe_acc[:, :, :], stats_m, mv_m, rstd_m, g("acc"), None, gb=2)
                y = dve.do(lambda e: e.tensor_tensor(y_out[p2][:, :, :], moe_acc[:, :, :], x1[p2][:, :, :], ALU.add), [y, g("stored", n - 2)])
                y = layer_norm(y_out[p2], y_out[p2][:, :, :], stats_m, mv_m, rstd_m, y, None)
                m["final", n] = y
                m["stored", n] = sp.dma(lambda e: e.dma_start(io["out"][:, n * T:(n + 1) * T, :].rearrange("b t c -> t b c"), y_out[p2][:, :, :]),
                                        s_y[p2], [y])
            steps = [start] + [up(0, f) for f in range(FT)]
            for x in range(NE):
                if x + 1 < NE:
                    steps += [up(x + 1, f) for f in range(FT)]
                steps.append(down(x))
            return steps + [finish]

        for step in project(0) + project(1):
            step()
        for step in conv_norm(0):
            step()
        for i in range(NBLK + 2):
            lanes = []
            if i < NBLK:
                lanes.append(prepare(i) + chunks(i))
            if i + 1 < NBLK:
                lanes.append((project(i + 2) if i + 2 < NBLK else []) + conv_norm(i + 1))
            if 0 <= i - 1 < NBLK:
                lanes.append(read_out(i - 1) + mixer_out(i - 1) + attention(i - 1) + gate(i - 1))
            if 0 <= i - 2 < NBLK:
                lanes.append(experts(i - 2))
            interleave(lanes)
        for n in (NBLK - 2, NBLK - 1):
            sp.wait(m["stored", n])

        names = [q.name for q in (pe, dve, act, pool, s_const, *s_x, *s_xt, *s_y)]
        sems = {name: ctx.enter_context(nc.semaphore(name)) for name in names}
        block = ctx.enter_context(nc.Block())

        @block.tensor
        def _(eng):
            pe.emit(eng, sems)

        @block.vector
        def _(eng):
            dve.emit(eng, sems)

        @block.scalar
        def _(eng):
            act.emit(eng, sems)

        @block.gpsimd
        def _(eng):
            pool.emit(eng, sems)

        @block.sync
        def _(eng):
            sp.emit(eng, sems)


def kernel(**inputs):
    import concourse.bacc as bacc
    from concourse.bass_utils import run_bass_kernel_spmd

    a = {k[3:]: np.asarray(v) for k, v in inputs.items()}
    x = a["attn_x"]

    def rows(v):
        return np.tile(v[None], (128,) + (1,) * v.ndim)

    halves = 2
    arrays = {
        "x": x,
        "x_ch": x.reshape(B, NBLK, T, C).transpose(3, 1, 0, 2),
        "w_qkv": np.stack([a["attn_Wq"].T, a["attn_Wk"].T, a["attn_Wv"].T], 1),
        "b_qkv": np.stack([a["attn_bq"], a["attn_bk"], a["attn_bv"]], 1),
        "w_gates": np.concatenate([a["attn_Wa"].T, a["attn_Wb"].T], 1),
        "b_gates": np.stack([np.tile(np.repeat(v, halves), B) for v in (a["attn_ba"], a["attn_bb"])], 1),
        "w_conv": np.stack([a["attn_conv_q"][:, 0], a["attn_conv_k"][:, 0], a["attn_conv_v"][:, 0]], 1),
        "w_o": a["attn_Wo"].T,
        "b_rows": np.stack([a["attn_bo"], a["ffn_out_b"]])[None],
        "w_in": a["ffn_in_proj_w"].T,
        "b_in": rows(a["ffn_in_proj_b"]),
        "w_out": a["ffn_out_w"].T,
        "w_gate": a["ffn_gate_w"].T,
        "b_gate": rows(a["ffn_gate_b"]),
        "w1": a["ffn_w1"].transpose(2, 0, 1),
        "b1": a["ffn_b1"].reshape(NE, FT, 128).transpose(2, 0, 1),
        "w2": a["ffn_w2"].reshape(NE, C, FT, 128).transpose(3, 0, 2, 1),
        "b2": a["ffn_b2"],
        "ln_gb": rows(np.stack([a["ffn_ln1_g"], a["ffn_ln1_b"], a["ffn_ln2_g"], a["ffn_ln2_b"]])),
        "ident": np.eye(128, dtype=np.float32),
        "fold": np.repeat(np.eye(B * H, dtype=np.float32), halves, axis=0),
        "tril": np.tile(np.tril(np.ones((NE, NE), np.float32), -1)[None], (128, 1, 1)),
    }
    arrays = {k: np.ascontiguousarray(v) for k, v in arrays.items()}
    nc = bacc.Bacc("TRN2", target_bir_lowering=False, num_devices=1)
    io = {k: nc.dram_tensor(f"in_{k}", v.shape, F32, kind="ExternalInput").ap() for k, v in arrays.items()}
    io["out"] = nc.dram_tensor("out", (B, N, C), F32, kind="ExternalOutput").ap()
    build(nc, io)
    r = run_bass_kernel_spmd(nc, [{f"in_{k}": v for k, v in arrays.items()}], core_ids=[0])
    return r.results[0]["out"]
```

```python
import concourse.bass as bass
from concourse import mybir
from contextlib import ExitStack
import numpy as np

F32 = mybir.dt.float32
ALU = mybir.AluOpType
ACT = mybir.ActivationFunctionType
AX = mybir.AxisListType

B = 4
N = 1024
C = 128
H = 16
E = C // H
TAPS = 4
PAD = TAPS // 2
T = 128
NBLK = N // T
J = 4
CH = T // J
G = 4
HC = CH // 2
DQ = E // 2
NE = 8
FF = 512
FT = FF // 128
L2_EPS = 1e-6
LN_EPS = 1e-5
SCALE = float(E) ** -0.5


class Mark:

    def __init__(self, owner):
        self.owner, self.value, self.done_at = owner, None, None


class Lane:

    def __init__(self):
        self.items = []


def free_size(ap):
    size = 1
    for x in ap.shape[1:]:
        size *= x
    return size


class Estimate:

    def __init__(self, fixed, per_column, pointer):
        self.fixed, self.per_column, self.pointer = fixed, per_column, pointer

    def of(self, ap, pointers=0):
        return self.fixed + self.per_column * free_size(ap) + self.pointer * pointers

    def matmul(self, out, lhsT, rhs, start, stop):
        return self.of(rhs) if free_size(rhs) > free_size(lhsT) else self.of(lhsT)

    def transpose(self, out, in_, identity):
        return 110

    def activation(self, out, in_, func, bias=None, scale=None, accum_out=None):
        return self.of(in_, (bias is not None) + (scale is not None and not isinstance(scale, float)))

    def tensor_tensor(self, out, in0, in1, op):
        return 950 if op == ALU.pow else self.of(out)

    def tensor_reduce(self, out, in_, axis, op):
        return self.of(in_)

    def tensor_scalar(self, out, in0, scalar1, scalar2, op0, op1=None):
        return self.fixed + self.per_column * free_size(out) / 2 + self.pointer * (not isinstance(scalar1, float))

    def scalar_tensor_tensor(self, out, in0, scalar, in1, op0, op1):
        return self.of(out, 1)

    def tensor_copy(self, out, in_):
        return self.of(out)

    def reciprocal(self, out, in_):
        return self.fixed + 6 * self.per_column * free_size(out)

    def bn_stats(self, out, in_):
        return self.of(in_)

    def bn_aggr(self, out, in_):
        return self.fixed

    def memset(self, out, value):
        return self.fixed

    def dma_start(self, out, in_):
        return 2000


class Queue:

    lane = Lane()

    def __init__(self, name, estimate, delay):
        self.name, self.items, self.count = name, [], 0
        self.estimate, self.delay, self.free_at = estimate, delay, 0

    def record(self, make, after, owner, step):
        mark = Mark(owner)
        Queue.lane.items.append((self, make, [m for m in after if m is not None], mark, step))
        return mark

    def do(self, make, after=()):
        return self.record(make, after, self, 1)

    def part(self, make, after=()):
        return self.record(make, after, self, 0)

    def dma(self, make, sem, after=()):
        return self.record(make, after, sem, 16)

    def wait(self, mark):
        self.record(None, [mark], self, 0)

    def starts_at(self, item):
        at = self.free_at
        for m in item[2]:
            if m.done_at is None:
                return None
            at = max(at, m.done_at)
        return at

    def place(self, item):
        _, make, _, mark, step = item
        cost = make(self.estimate) if make else 0
        start = self.starts_at(item)
        self.free_at = start + (50 if step == 16 else cost)
        mark.done_at = start + cost + self.delay
        mark.owner.count += step
        mark.value = mark.owner.count
        self.items.append(item)

    def emit(self, eng, sems):
        seen = {}
        for _, make, after, mark, step in self.items:
            for m in after:
                name = m.owner.name
                if seen.get(name, 0) < m.value:
                    eng.wait_ge(sems[name], m.value)
                    seen[name] = m.value
            if make is not None:
                ins = make(eng)
                if step:
                    ins.then_inc(sems[mark.owner.name], step)


class DmaSem:
    def __init__(self, name):
        self.name, self.count = name, 0


class Banks:

    def __init__(self, aps):
        self.aps, self.freed, self.at = aps, [None] * len(aps), 0

    def take(self):
        i = self.at
        self.at = (i + 1) % len(self.aps)
        return i, self.aps[i], self.freed[i]


def record(steps):
    Queue.lane = Lane()
    for step in steps:
        step()
    return Queue.lane.items


def interleave(lanes):
    streams = []
    for lane in lanes:
        by_queue = {}
        for item in lane:
            by_queue.setdefault(item[0].name, []).append(item)
        streams += by_queue.values()
    at = [0] * len(streams)
    while True:
        best = None
        for w, stream in enumerate(streams):
            if at[w] < len(stream):
                start = stream[at[w]][0].starts_at(stream[at[w]])
                if start is not None and (best is None or start < best[0]):
                    best = (start, w)
        if best is None:
            break
        w = best[1]
        streams[w][at[w]][0].place(streams[w][at[w]])
        at[w] += 1
    assert at == [len(stream) for stream in streams], "something waits for what is never placed"


def build(nc, io):
    ctx = ExitStack()

    def sb(name, shape):
        return ctx.enter_context(nc.sbuf_tensor(name, shape, F32))

    with ctx:
        pe = Queue("pe", Estimate(0, 1.12 * 4 / 2.4, 0), 200)
        dve = Queue("dve", Estimate(69, 1.042, 64), 130)
        act = Queue("act", Estimate(93, 0.833, 60), 235)
        pool = Queue("pool", Estimate(60, 2.1, 0), 65)
        sp = Queue("sp", Estimate(0, 0, 0), 0)

        w_qkv = sb("w_qkv", [C, 3, C])
        b_qkv = sb("b_qkv", [C, 3])
        w_gates = sb("w_gates", [C, 2 * H])
        b_gates = sb("b_gates", [128, 2])
        w_conv = sb("w_conv", [C, 3, TAPS])
        w_o = sb("w_o", [C, C])
        b_rows = sb("b_rows", [1, 2, C])
        w_in = sb("w_in", [C, 3 * C])
        b_in = sb("b_in", [128, 3 * C])
        w_out = sb("w_out", [C, C])
        w_gate = sb("w_gate", [C, NE])
        b_gate = sb("b_gate", [128, NE])
        w1 = sb("w1", [C, NE, FF])
        b1 = sb("b1", [128, NE, FT])
        w2 = sb("w2", [128, NE, FT, C])
        b2 = sb("b2", [NE, C])
        ln_gb = sb("ln_gb", [128, 4, C])
        ident = sb("ident", [128, 128])
        fold = sb("fold", [128, B * H])
        tril = sb("tril", [128, NE, NE])
        ones = sb("ones", [1, 128])

        NX = 3
        x_ch = [sb(f"x_ch{i}", [C, B, T]) for i in range(2)]
        x_tok = sb("x_tok", [T, B, C])
        proj = [sb(f"proj{i}", [C, 3, B, T + TAPS - 1]) for i in range(2)]
        conv_acc = sb("conv_acc", [C, B, T])
        conv_out = [sb(f"conv_out{i}", [C, B, T]) for i in range(2)]
        gates_tok = sb("gates_tok", [T, 2, B * H, 2])
        sq_junk = sb("sq_junk", [T, C])
        sqrt_power = sb("sqrt_power", [128, 2, B])
        ssq = sb("ssq", [T, 2, B])
        q_tok = sb("q_tok", [T, B, C])
        v_tok = sb("v_tok", [T, B, C])
        k_tok = sb("k_tok", [T, B * H, 2, E])
        k_w = [sb(f"k_w{i}", [128, T, E]) for i in range(3)]
        v_w = [sb(f"v_w{i}", [128, T, DQ]) for i in range(2)]
        q_w = [sb(f"q_w{i}", [128, T, DQ]) for i in range(3)]
        ab_w = [sb(f"ab_w{i}", [128, 2, T]) for i in range(2)]
        decay = [sb(f"decay{i}", [128, T]) for i in range(2)]
        ratio = [sb(f"ratio{i}", [128, CH, 3, J]) for i in range(2)]
        bratio = sb("bratio", [128, CH, 3, J])
        kk_prod = sb("kk_prod", [128, HC, J - 1, E])
        lmat = sb("lmat", [128, HC, 3, J])
        bdecay = sb("bdecay", [128, T])
        solve = [sb(f"solve{i}", [128, HC, J, E + DQ]) for i in range(2)]
        solve_t = sb("solve_t", [128, HC, E + DQ])
        kend = [sb(f"kend{i}", [128, HC, J, E]) for i in range(2)]
        eend = sb("eend", [128, CH, J])
        sk_buf = sb("sk_buf", [128, 2, G, J * DQ, E + 1])
        uk_buf = [sb(f"uk_buf{i}", [128, DQ * E, J + 1]) for i in range(2)]
        u_neg = [sb(f"u_neg{i}", [128, CH, J, DQ]) for i in range(2)]
        state = [sb(f"state{i}", [128, CH, E, DQ]) for i in range(2)]
        read_prod = [sb(f"read_prod{i}", [128, CH, E, DQ]) for i in range(2)]
        q_decay = sb("q_decay", [128, T, DQ])
        o_w = sb("o_w", [128, CH, J, E])
        uq = sb("uq", [128, CH, J])
        uq_prod = sb("uq_prod", [128, CH, J, DQ])
        ch_a = sb("ch_a", [C, B, T])
        ch_x = [sb(f"ch_x{i}", [C, B, T]) for i in range(2)]
        x1 = [sb(f"x1_{i}", [T, B, C]) for i in range(2)]
        x2 = [sb(f"x2_{i}", [T, B, C]) for i in range(2)]
        stats = sb("stats", [T, B, 6])
        mv = sb("mv", [T, B, 2])
        rstd = sb("rstd", [T, B])
        stats_m = sb("stats_m", [T, B, 6])
        mv_m = sb("mv_m", [T, B, 2])
        rstd_m = sb("rstd_m", [T, B])
        attn_in = sb("attn_in", [T, B, 3 * C])
        tok_tmp = [sb(f"tok_tmp{i}", [T, B, C]) for i in range(2)]
        score = sb("score", [T, B, H, B])
        smax = sb("smax", [T, B, H])
        logit = sb("logit", [T, B, NE])
        lmax = sb("lmax", [T, B])
        rank = sb("rank", [T, B, NE])
        combine = [sb(f"combine{i}", [T, B, NE]) for i in range(2)]
        combine_t = [sb(f"combine_t{i}", [NE, B, T]) for i in range(2)]
        hidden = sb("hidden", [128, 2 * FT, B * T])
        moe_acc = sb("moe_acc", [T, B, C])
        y_out = sb("y_out", [T, B, C])

        ps = [ctx.enter_context(nc.psum_tensor(f"ps{i}", [128, 512], F32)) for i in range(8)]
        banks_a, banks_p, banks_h, banks_y = Banks(ps[0:2]), Banks(ps[2:4]), Banks(ps[4:6]), Banks(ps[6:8])

        s_first, s_const, s_moe = DmaSem("s_first"), DmaSem("s_const"), DmaSem("s_moe")
        s_x = [DmaSem(f"s_x{i}") for i in range(2)]
        s_xt = [DmaSem(f"s_xt{i}") for i in range(2)]
        s_y = [DmaSem(f"s_y{i}") for i in range(2)]

        def load(dst, name, sem=s_const):
            src = io[name]
            return sp.dma(lambda e: e.dma_start(dst, src), sem)

        def load_x_ch(n, after=()):
            return sp.dma(lambda e: e.dma_start(x_ch[n % 2][:, :, :], io["x_ch"][:, n, :, :]), s_x[n % 2], after)

        Queue.lane = Lane()
        x_ch_loaded = {0: load_x_ch(0)}
        load(w_qkv[:, :, :], "w_qkv", s_first)
        load(b_qkv[:, :], "b_qkv", s_first)
        load(w_gates[:, :], "w_gates", s_first)
        load(b_gates[:, :], "b_gates", s_first)
        load(w_conv[:, :, :], "w_conv", s_first)
        first_loaded = load(ident[:, :], "ident", s_first)
        x_ch_loaded[1] = load_x_ch(1)
        load(fold[:, :], "fold")
        load(w_o[:, :], "w_o")
        load(b_rows[:, :, :], "b_rows")
        load(w_in[:, :], "w_in")
        load(b_in[:, :], "b_in")
        load(w_out[:, :], "w_out")
        load(w_gate[:, :], "w_gate")
        load(b_gate[:, :], "b_gate")
        load(tril[:, :, :], "tril")
        mix_loaded = load(ln_gb[:, :, :], "ln_gb")
        load(b1[:, :, :], "b1", s_moe)
        load(b2[:, :], "b2", s_moe)
        load(w1[:, :, :], "w1", s_moe)
        moe_loaded = load(w2[:, :, :, :], "w2", s_moe)

        ones_set = pool.do(lambda e: e.memset(ones[:, :], 1.0))
        pool.do(lambda e: e.memset(sqrt_power[:, 0, :], 0.5))
        power_set = pool.do(lambda e: e.memset(sqrt_power[:, 1, :], -0.5))
        front_set = pool.do(lambda e: e.memset(proj[0][:, :, :, 0:PAD], 0.0))
        state_set = pool.do(lambda e: e.memset(state[0][:, 0, :, :], 0.0))

        prologue = Queue.lane.items
        m = {}

        def g(*key):
            return m.get(key)

        def spare(n, idle):
            return dve if n == idle else pool

        def project(n):
            def proj_one(k):
                def run():
                    i, bank, freed = banks_a.take()
                    mm = pe.do(lambda e: e.matmul(bank[:, :], w_qkv[:, k, :], x_ch[n % 2][:, :, :].rearrange("c b t -> c (b t)"),
                                                  start=True, stop=True),
                               [first_loaded, x_ch_loaded[n], freed])
                    here, there = proj[n % 2], proj[1 - n % 2]
                    banks_a.freed[i] = act.do(
                        lambda e: e.activation(here[:, k, :, PAD:PAD + T], bank[:, :].rearrange("c (b t) -> c b t", b=B), ACT.Silu, bias=b_qkv[:, k:k + 1]),
                        [mm, first_loaded, g("conv", n - 2, k)])
                    done = banks_a.freed[i]
                    if n:
                        done = act.do(lambda e: e.activation(there[:, k, :, PAD + T:], here[:, k, :, PAD:PAD + 1], ACT.Copy), [done])
                    m["proj", n, k] = done
                return run

            def gate_mm():
                i, bank, freed = banks_a.take()
                for b in range(B):
                    dst = bank[:, 0:2 * B * H].rearrange("t (k b h) -> t b k h", k=2, b=B)[:, b, :, :]
                    mk = (pe.do if b == B - 1 else pe.part)(
                        lambda e, b=b, dst=dst: e.matmul(dst, x_ch[n % 2][:, b, :], w_gates[:, :].rearrange("c (k h) -> c k h", k=2),
                                                         start=True, stop=True),
                        [first_loaded, x_ch_loaded[n], freed])
                ev = dve.do(lambda e, bank=bank: e.tensor_copy(
                    gates_tok[:, :, :, :],
                    bank[:, 0:2 * B * H].rearrange("t (k g) -> t k g", k=2).unsqueeze(3).to_broadcast([T, 2, B * H, 2])), [mk, g("gate_t", n - 1)])
                banks_a.freed[i] = ev
                m["x_ch_read", n] = mk
                if n + 2 < NBLK:
                    x_ch_loaded[n + 2] = load_x_ch(n + 2, [mk])
                i, bank, freed = banks_a.take()
                pe.part(lambda e: e.transpose(bank[:, 0:T], gates_tok[:, 0, :, :].rearrange("t g d -> t (g d)"), ident[:, :]), [ev, freed])
                tr = pe.do(lambda e: e.transpose(bank[:, T:2 * T], gates_tok[:, 1, :, :].rearrange("t g d -> t (g d)"), ident[:, :]))
                m["gate_t", n] = tr
                for k in range(2):
                    banks_a.freed[i] = act.do(
                        lambda e, k=k: e.activation(ab_w[n % 2][:, k, :], bank[:, k * T:(k + 1) * T], ACT.Sigmoid, bias=b_gates[:, k:k + 1]),
                        [tr, g("prep_done", n - 2)])
                m["ab", n] = banks_a.freed[i]
            return [proj_one(0), proj_one(1), proj_one(2)], [gate_mm]

        def conv_norm(n):
            ahead = min(n + 1, NBLK - 1)
            steps = []

            def conv_one(k):
                def run():
                    done, back = g("proj", ahead, k), None
                    here, there = proj[n % 2], proj[1 - n % 2]
                    src = [here[:, k, :, j:j + T] for j in range(TAPS)]
                    if n + 1 == NBLK:
                        back = pool.do(lambda e: e.memset(here[:, k, :, PAD + T:], 0.0), [done, g("conv", n - 2, k)])
                    a = dve.do(lambda e: e.tensor_scalar(conv_acc[:, :, :], src[0], w_conv[:, k, 0:1], None, ALU.mult),
                               [done, front_set, first_loaded, g("conv_silu"), g("front", n, k), back])
                    for j in range(1, TAPS):
                        a = dve.do(lambda e, j=j: e.scalar_tensor_tensor(conv_acc[:, :, :], src[j], w_conv[:, k, j:j + 1],
                                                                         conv_acc[:, :, :], ALU.mult, ALU.add), [a])
                    m["conv", n, k] = a
                    if n + 1 < NBLK:
                        m["front", n + 1, k] = act.do(lambda e: e.activation(there[:, k, :, 0:PAD], here[:, k, :, T:T + PAD], ACT.Copy), [a])
                    dst = conv_out[k % 2]
                    s = act.do(lambda e: e.activation(dst[:, :, :], conv_acc[:, :, :], ACT.Silu), [a, g("conv_out_read", k % 2)])
                    m["conv_silu",] = s
                    i, bank, freed = banks_a.take()
                    for b in range(B):
                        tr = (pe.do if b == B - 1 else pe.part)(
                            lambda e, b=b: e.transpose(bank[:, b * C:(b + 1) * C], dst[:, b, :], ident[:, :]), [s, freed])
                    m["conv_out_read", k % 2] = tr
                    if k == 2:
                        banks_a.freed[i] = act.do(lambda e: e.activation(v_tok[:, :, :].rearrange("t b c -> t (b c)"), bank[:, :], ACT.Copy),
                                                  [tr, g("v_tok_read")])
                        m["v_tok", n] = banks_a.freed[i]
                    else:
                        for b in range(B):
                            sq = act.do(lambda e, b=b: e.activation(sq_junk[:, :], bank[:, b * C:(b + 1) * C], ACT.Square,
                                                                    accum_out=ssq[:, k, b:b + 1]), [tr, g("ssq_read", k), g("sq_prev")])
                            m["sq_prev",] = sq
                        nrm = pool.do(lambda e: e.tensor_tensor(ssq[:, k, :], ssq[:, k, :], sqrt_power[:, 0, :], ALU.pow), [sq, power_set])
                        ad = dve.do(lambda e: e.tensor_scalar(ssq[:, k, :], ssq[:, k, :], L2_EPS, None, ALU.add), [nrm])
                        rc = dve.do(lambda e: e.reciprocal(ssq[:, k, :], ssq[:, k, :]), [ad])
                        out = k_tok[:, :, 0, :].rearrange("t (b h) e -> t b h e", b=B) if k else q_tok[:, :, :].rearrange("t b (h e) -> t b h e", e=E)
                        banks_a.freed[i] = dve.do(lambda e: e.tensor_tensor(
                            out, bank[:, :].rearrange("t (b h e) -> t b h e", b=B, e=E),
                            ssq[:, k, :].unsqueeze(2).unsqueeze(3).to_broadcast([T, B, H, E]), ALU.mult),
                            [rc, tr, g(("q_tok_read", "k_tok_read")[k])])
                        m["ssq_read", k] = banks_a.freed[i]
                        m[("q_tok", "k_tok")[k], n] = banks_a.freed[i]
                        if k:
                            m["k_tok", n] = act.do(lambda e: e.activation(k_tok[:, :, 1, :], k_tok[:, :, 0, :], ACT.Copy), [banks_a.freed[i]])
                return run

            def to_state(k):
                def run():
                    tok = (q_tok, None, v_tok)[k]
                    name = ("q", "k", "v")[k]
                    dst, old = ((q_w[n % 3], g("o_done", n - 3)), (k_w[n % 3], g("o_done", n - 3)), (v_w[n % 2], g("prep_done", n - 2)))[k]
                    for half in range(2 if k == 1 else 1):
                        i, bank, freed = banks_a.take()
                        for d in range(4):
                            if k == 1:
                                src = k_tok[:, :, :, :].rearrange("t g s e -> t (g s) e")[:, :, 4 * half + d]
                            else:
                                src = tok[:, :, :].rearrange("t b (g d) -> t (b g) d", d=DQ)[:, :, d]
                            tr = (pe.do if d == 3 else pe.part)(
                                lambda e, d=d, src=src, bank=bank: e.transpose(bank[:, d * T:(d + 1) * T], src, ident[:, :]),
                                [g(name + "_tok", n), freed])
                        out = dst[:, :, 4 * half:4 * half + 4].rearrange("p t d -> p d t") if k == 1 else dst[:, :, :].rearrange("p t d -> p d t")
                        banks_a.freed[i] = act.do(lambda e, out=out, bank=bank: e.activation(
                            out, bank[:, :].rearrange("p (d t) -> p d t", d=4), ACT.Copy), [tr, old])
                    m[name + "_w", n] = banks_a.freed[i]
                    m[name + "_tok_read",] = tr
                return run
            return [conv_one(0), to_state(0), conv_one(1), to_state(1), conv_one(2), to_state(2)]

        def chunked(ap):
            return ap.rearrange("p (c j) -> p c j", j=J)

        def prepare(n):
            p2, p3 = n % 2, n % 3

            def decays():
                a, b = chunked(ab_w[p2][:, 0, :]), chunked(ab_w[p2][:, 1, :])
                dec = chunked(decay[p2][:, :])
                rat = ratio[p2]
                x = dve.do(lambda e: e.tensor_copy(dec[:, :, 0], a[:, :, 0]), [g("ab", n), g("o_done", n - 2)])
                for j in range(1, J):
                    x = dve.do(lambda e, j=j: e.tensor_tensor(dec[:, :, j], dec[:, :, j - 1], a[:, :, j], ALU.mult), [x])
                y = dve.do(lambda e: e.tensor_copy(rat[:, :, 0, 1:J], a[:, :, 1:J]))
                for lag in range(2, J):
                    y = dve.do(lambda e, lag=lag: e.tensor_tensor(rat[:, :, lag - 1, lag:J], rat[:, :, lag - 2, lag:J],
                                                                  a[:, :, 1:J - lag + 1], ALU.mult), [y])
                z = x
                for lag in range(1, J):
                    z = dve.do(lambda e, lag=lag: e.tensor_tensor(bratio[:, :, lag - 1, lag:J], rat[:, :, lag - 1, lag:J],
                                                                  b[:, :, lag:J], ALU.mult), [y])
                w = dve.do(lambda e: e.tensor_tensor(bdecay[:, :], decay[p2][:, :], ab_w[p2][:, 1, :], ALU.mult), [x, g("sub")])
                s = dve.do(lambda e: e.memset(eend[:, :, J - 1], -1.0), [g("kend")])
                for lag in range(1, J):
                    s = dve.do(lambda e, lag=lag: e.tensor_scalar(eend[:, :, J - 1 - lag], rat[:, :, lag - 1, J - 1], -1.0, None, ALU.mult), [y])
                m["decays", n], m["bratio", n], m["bdecay", n] = s, z, w

            def half(h):
                c0 = HC * h
                k = k_w[p3][:, c0 * J:(c0 + HC) * J, :]
                v = v_w[p2][:, c0 * J:(c0 + HC) * J, :]
                kc = k.rearrange("p (c j) e -> p c j e", j=J)
                sol, ke = solve[h], kend[h]

                def over_steps(ap, width):
                    return ap.unsqueeze(2).to_broadcast([128, HC * J, width])

                def rhs():
                    r1 = spare(n, 0).do(lambda e: e.tensor_tensor(sol[:, :, :, 0:E].rearrange("p c j e -> p (c j) e"), k,
                                                           over_steps(bdecay[:, c0 * J:(c0 + HC) * J], E), ALU.mult),
                                 [g("bdecay", n), g("k_w", n), g("half_done", n - 1, h)])
                    r2 = spare(n, 0).do(lambda e: e.tensor_tensor(sol[:, :, :, E:].rearrange("p c j d -> p (c j) d"), v,
                                                           over_steps(ab_w[p2][:, 1, c0 * J:(c0 + HC) * J], DQ), ALU.mult),
                                 [g("ab", n), g("v_w", n), g("laid", n - 1, (h + 1) * HC // G - 1)])
                    m["rhs", n, h] = r2

                def k_end():
                    m["kend", n, h] = m["kend",] = spare(n, 0).do(
                        lambda e: e.tensor_tensor(ke[:, :, :, :].rearrange("p c j e -> p (c j) e"), k,
                                                  over_steps(eend[:, c0:c0 + HC, :].rearrange("p c j -> p (c j)"), E), ALU.mult),
                        [g("decays", n), g("k_w", n), g("half_done", n - 1, h)])

                def dots(lag):
                    def run():
                        prod = kk_prod[:, :, 0:J - lag, :]
                        x = spare(n, 0).do(lambda e: e.tensor_tensor(prod, kc[:, :, lag:J, :], kc[:, :, 0:J - lag, :], ALU.mult), [g("k_w", n), g("kk_read")])
                        x = dve.do(lambda e: e.tensor_reduce(lmat[:, :, lag - 1, lag:J], prod, AX.X, ALU.add), [x, g("sub")])
                        m["kk_read",] = x
                        m["lmat", n, h] = dve.do(lambda e: e.tensor_tensor(lmat[:, :, lag - 1, lag:J], lmat[:, :, lag - 1, lag:J],
                                                                           bratio[:, c0:c0 + HC, lag - 1, lag:J], ALU.mult), [x, g("bratio", n)])
                    return run

                def substitute(j, i):
                    def run():
                        x = spare(n, 0).do(lambda e: e.tensor_tensor(solve_t[:, :, :], sol[:, :, i, :],
                                                              lmat[:, :, j - i - 1, j].unsqueeze(2).to_broadcast([128, HC, E + DQ]), ALU.mult),
                                    [g("lmat", n, h), g("rhs", n, h), g("sub")])
                        m["sub",] = m["prep", n, h] = spare(n, 0).do(lambda e: e.tensor_tensor(sol[:, :, j, :], sol[:, :, j, :], solve_t[:, :, :], ALU.subtract), [x])
                        m["prep_done", n] = m["sub",]
                    return run
                return [dots(lag) for lag in range(1, J)] + [rhs] + [substitute(j, i) for j in range(1, J) for i in range(j)] + [k_end]
            return [decays] + half(0) + half(1)

        def chunks(n):
            p2 = n % 2

            def lay_u0(q):
                m["laid", n, q] = act.do(lambda e: e.activation(
                    sk_buf[:, q % 2, :, :, E].rearrange("p c (j d) -> p c j d", j=J),
                    solve[G * q // HC][:, G * q % HC:G * q % HC + G, :, E:], ACT.Copy, scale=-1.0),
                    [g("prep", n, G * q // HC), g("laid_read", q % 2)])

            def one(c):
                def run():
                    if c == 0:
                        lay_u0(0)
                    if c % G == 0 and c + G < CH:
                        lay_u0(c // G + 1)
                    s_in = state[p2][:, c, :, :]
                    s_out = state[p2][:, c + 1, :, :] if c + 1 < CH else state[1 - p2][:, 0, :, :]
                    half = c // HC
                    w = solve[half][:, c % HC, :, 0:E]
                    sk = sk_buf[:, c // G % 2, c % G, :, :]
                    un = u_neg[p2][:, c, :, :]
                    uk = uk_buf[c % 2]
                    aged = act.do(lambda e: e.activation(uk[:, :, J], s_in.rearrange("p e d -> p (e d)"), ACT.Copy,
                                                         scale=decay[p2][:, c * J + J - 1:c * J + J]), [state_set, g("state"), g("decays", n), g("aged_read", c % 2)])
                    x = dve.do(lambda e: e.tensor_tensor(
                        sk[:, :, 0:E].rearrange("p (j d) e -> p j d e", j=J), s_in.rearrange("p e d -> p d e").unsqueeze(1).to_broadcast([128, J, DQ, E]),
                        w.unsqueeze(2).to_broadcast([128, J, DQ, E]), ALU.mult), [state_set, g("state"), g("prep", n, half), g("o_done", n - 2)])
                    x = dve.do(lambda e: e.tensor_reduce(un.rearrange("p j d -> p (j d)"), sk, AX.X, ALU.add), [x, g("laid", n, c // G), g("o_done", n - 2)])
                    m["laid_read", c // G % 2] = x
                    x = dve.do(lambda e: e.tensor_tensor(
                        uk[:, :, 0:J].rearrange("p (e d) j -> p e d j", d=DQ), un.rearrange("p j d -> p d j").unsqueeze(1).to_broadcast([128, E, DQ, J]),
                        kend[half][:, c % HC, :, :].rearrange("p j e -> p e j").unsqueeze(2).to_broadcast([128, E, DQ, J]), ALU.mult), [x, g("kend", n, half)])
                    m["state",] = dve.do(lambda e: e.tensor_reduce(s_out.rearrange("p e d -> p (e d)"), uk[:, :, :], AX.X, ALU.add),
                                         [x, aged, g("o_done", n - 1) if c + 1 == CH else None])
                    m["aged_read", c % 2] = m["state",]
                    if (c + 1) % HC == 0:
                        m["half_done", n, half] = m["state",]
                    if c + 1 == CH:
                        m["chunks", n] = m["state",]
                return run
            return [one(c) for c in range(CH)]

        def read_out(n):
            p2, p3 = n % 2, n % 3
            qc = q_w[p3][:, :, :].rearrange("p (c j) d -> p c j d", j=J)
            kc = k_w[p3][:, :, :].rearrange("p (c j) e -> p c j e", j=J)

            def decayed_q():
                m["q_decay",] = spare(n, NBLK - 1).do(lambda e: e.tensor_tensor(q_decay[:, :, :], q_w[p3][:, :, :], decay[p2][:, :].unsqueeze(2).to_broadcast([128, T, DQ]),
                                                                  ALU.mult), [g("q_w", n), g("chunks", n)])

            def from_state(j):
                def run():
                    qd = q_decay[:, :, :].rearrange("p (c j) d -> p c j d", j=J)
                    buf = read_prod[j % 2]
                    x = spare(n, NBLK - 1).do(lambda e: e.tensor_tensor(
                        buf[:, :, :, :], state[p2][:, :, :, :],
                        qd[:, :, j, :].unsqueeze(2).to_broadcast([128, CH, E, DQ]), ALU.mult), [g("q_decay"), g("read_red", j % 2)])
                    m["read_red", j % 2] = m["o_w",] = dve.do(lambda e: e.tensor_reduce(o_w[:, :, j, :], buf[:, :, :, :], AX.X, ALU.add), [x, g("o_w_read")])
                return run

            def lag_part(lag):
                def run():
                    w = J - lag
                    buf = read_prod[lag % 2]
                    prod = buf[:, :, :, :].rearrange("p c e d -> p c (e d)").rearrange("p c (j e) -> p c j e", j=J)[:, :, 0:w, :]
                    x = dve.do(lambda e: e.tensor_tensor(uq_prod[:, :, 0:w, :], qc[:, :, lag:J, :], u_neg[p2][:, :, 0:w, :], ALU.mult), [g("uq")])
                    x = dve.do(lambda e: e.tensor_reduce(uq[:, :, 0:w], uq_prod[:, :, 0:w, :], AX.X, ALU.add), [x, g("ow")])
                    if lag:
                        x = dve.do(lambda e: e.tensor_tensor(uq[:, :, 0:w], uq[:, :, 0:w], ratio[p2][:, :, lag - 1, lag:J], ALU.mult), [x])
                    m["uq",] = x
                    m["ow",] = spare(n, NBLK - 1).do(lambda e: e.tensor_tensor(prod, kc[:, :, 0:w, :],
                                                                 uq[:, :, 0:w].unsqueeze(3).to_broadcast([128, CH, w, E]), ALU.mult),
                                       [x, g("read_red", lag % 2)])
                    m["read_red", lag % 2] = m["o_w",] = spare(n, NBLK - 1).do(lambda e: e.tensor_tensor(o_w[:, :, lag:J, :], o_w[:, :, lag:J, :], prod, ALU.subtract),
                                                                 [g("ow"), g("o_w")])
                    if lag == J - 1:
                        m["o_done", n] = m["o_w",]
                return run
            return [decayed_q] + [from_state(j) for j in range(J)] + [lag_part(lag) for lag in range(J)]

        def transpose4(banks, src, dst, after, old):
            i, bank, freed = banks.take()
            for b in range(B):
                tr = (pe.do if b == B - 1 else pe.part)(
                    lambda e, b=b: e.transpose(bank[:, b * 128:(b + 1) * 128], src[:, b, :], ident[:, :]), [after, freed, mix_loaded])
            banks.freed[i] = act.do(lambda e: e.activation(dst.rearrange("c b t -> c (b t)"), bank[:, :], ACT.Copy), [tr, old])
            return tr, banks.freed[i]

        def dense(banks, src, w, bias_row, after):
            i, bank, freed = banks.take()
            for b in range(B):
                pe.part(lambda e, b=b: e.matmul(bank[:, b * C:(b + 1) * C], src[:, b, :], w, start=True, stop=False), [after, freed, mix_loaded])
                mm = (pe.do if b == B - 1 else pe.part)(
                    lambda e, b=b: e.matmul(bank[:, b * C:(b + 1) * C], ones[:, :], bias_row, start=False, stop=True), [ones_set])
            return i, bank, mm

        def layer_norm(src, dst, st, mvt, rs, after, old, gb=None):
            for b in range(B):
                x = dve.do(lambda e, b=b: e.bn_stats(st[:, b, :], src[:, b, :]), [after])
            for b in range(B):
                y = dve.do(lambda e, b=b: e.bn_aggr(mvt[:, b, :], st[:, b, :]), [x])
            s = dve.do(lambda e: e.tensor_scalar(rs[:, :], mvt[:, :, 1], LN_EPS, None, ALU.add), [y])
            r = pool.do(lambda e: e.tensor_tensor(rs[:, :], rs[:, :], sqrt_power[:, 1, :], ALU.pow), [s, power_set])
            for b in range(B):
                z = dve.do(lambda e, b=b: e.tensor_scalar(dst[:, b, :], src[:, b, :], mvt[:, b, 0:1], rs[:, b:b + 1], ALU.subtract, ALU.mult), [r, old])
            if gb is not None:
                for k, op in ((0, ALU.mult), (1, ALU.add)):
                    z = pool.do(lambda e, k=k, op=op: e.tensor_tensor(dst, dst, ln_gb[:, gb + k, :].unsqueeze(1).to_broadcast([T, B, C]), op),
                               [z, mix_loaded])
            return z

        def mixer_out(n):
            p2 = n % 2

            def load_tok():
                m["x_tok", n] = sp.dma(lambda e: e.dma_start(x_tok[:, :, :], io["x"][:, n * T:(n + 1) * T, :].rearrange("b t c -> t b c")),
                                       s_xt[p2], [g("x_tok_read", n - 1)])

            def fold_halves():
                i, bank, freed = banks_p.take()
                ow = o_w[:, :, :, :].rearrange("p c j e -> p (c j) e")
                out = bank[:, :].rearrange("t (g e) -> t g e", e=E)
                for x in range(E):
                    mm = (pe.do if x == E - 1 else pe.part)(
                        lambda e, x=x: e.matmul(out[:, :, x], ow[:, :, x], fold[:, :], start=True, stop=True), [g("o_done", n), freed, mix_loaded])
                m["o_w_read",] = mm
                banks_p.freed[i] = act.do(lambda e: e.activation(tok_tmp[0][:, :, :].rearrange("t b c -> t (b c)"), bank[:, :], ACT.Copy), [mm, g("tmp_free", 0)])
                m["o_tok",] = banks_p.freed[i]

            def to_ch():
                m["tmp_free", 0], m["ch_a",] = transpose4(banks_p, tok_tmp[0], ch_a[:, :, :], g("o_tok"), g("ch_a_read"))

            def out_proj():
                i, bank, mm = dense(banks_p, ch_a, w_o[:, :], b_rows[:, 0, :], g("ch_a"))
                m["ch_a_read",] = mm
                banks_p.freed[i] = dve.do(lambda e: e.tensor_tensor(x1[p2][:, :, :], bank[:, :].rearrange("t (b c) -> t b c", b=B), x_tok[:, :, :], ALU.add),
                                          [mm, g("x_tok", n), g("final", n - 2)])
                m["x_tok_read", n] = banks_p.freed[i]
                m["x1", n] = layer_norm(x1[p2], x1[p2][:, :, :], stats, mv, rstd, banks_p.freed[i], None)

            def x1_ch():
                _, m["x1_ch",] = transpose4(banks_p, x1[p2], ch_a[:, :, :], g("x1", n), g("ch_a_read"))
            return [load_tok, fold_halves, to_ch, out_proj, x1_ch]

        def attention(n):
            p2 = n % 2

            def in_proj(b):
                def run():
                    i, bank, freed = banks_p.take()
                    mm = pe.do(lambda e: e.matmul(bank[:, 0:3 * C], ch_a[:, b, :], w_in[:, :], start=True, stop=True), [g("x1_ch"), freed])
                    banks_p.freed[i] = dve.do(lambda e: e.tensor_tensor(attn_in[:, b, :], bank[:, 0:3 * C], b_in[:, :], ALU.add), [mm])
                    m["ch_a_read",] = mm
                    m["attn_in",] = banks_p.freed[i]
                return run

            def scores(s):
                def run():
                    tmp = tok_tmp[s % 2]
                    x = spare(n, NBLK - 1).do(lambda e: e.tensor_tensor(tmp[:, :, :], attn_in[:, s, 0:C].unsqueeze(1).to_broadcast([T, B, C]), attn_in[:, :, C:2 * C], ALU.mult),
                                [g("attn_in"), g("tmp_free", s % 2)])
                    m["tmp_free", s % 2] = m["scores",] = dve.do(lambda e: e.tensor_reduce(
                        score[:, s, :, :].rearrange("t h u -> t u h"), tmp[:, :, :].rearrange("t u (h e) -> t u h e", e=E), AX.X, ALU.add), [x, g("ctx")])
                return run

            def softmax():
                sc = score[:, :, :, :].rearrange("t s h u -> t (s h) u")
                mx = smax[:, :, :].rearrange("t s h -> t (s h)")
                bc = mx.unsqueeze(2).to_broadcast([T, B * H, B])
                x = dve.do(lambda e: e.tensor_reduce(mx, sc, AX.X, ALU.max), [g("scores")])
                x = dve.do(lambda e: e.tensor_tensor(sc, sc, bc, ALU.subtract), [x])
                x = act.do(lambda e: e.activation(sc, sc, ACT.Exp, scale=SCALE), [x])
                x = dve.do(lambda e: e.tensor_reduce(mx, sc, AX.X, ALU.add), [x])
                x = dve.do(lambda e: e.reciprocal(mx, mx), [x])
                m["attn",] = dve.do(lambda e: e.tensor_tensor(sc, sc, bc, ALU.mult), [x])

            bank_ctx = {}

            def context(s):
                def run():
                    tmp = tok_tmp[s % 2]
                    if s == 0:
                        bank_ctx["i"], bank_ctx["bank"], bank_ctx["freed"] = banks_p.take()
                    bank = bank_ctx["bank"]
                    x = spare(n, NBLK - 1).do(lambda e: e.tensor_tensor(
                        tmp[:, :, :].rearrange("t u (h e) -> t u h e", e=E),
                        score[:, s, :, :].rearrange("t h u -> t u h").unsqueeze(3).to_broadcast([T, B, H, E]),
                        attn_in[:, :, 2 * C:3 * C].rearrange("t u (h e) -> t u h e", e=E), ALU.mult), [g("attn"), g("tmp_free", s % 2)])
                    for u in range(B):
                        mm = (pe.do if u == B - 1 else pe.part)(
                            lambda e, u=u: e.matmul(bank[:, s * T:(s + 1) * T], tmp[:, u, :], ident[:, :], start=u == 0, stop=u == B - 1),
                            [x, bank_ctx["freed"], mix_loaded])
                    m["tmp_free", s % 2] = mm
                    m["ctx",] = x
                    if s == B - 1:
                        banks_p.freed[bank_ctx["i"]] = m["ch_a",] = act.do(
                            lambda e: e.activation(ch_a[:, :, :].rearrange("c b t -> c (b t)"), bank[:, :], ACT.Copy), [mm, g("ch_a_read")])
                return run

            def out_proj():
                i, bank, mm = dense(banks_p, ch_a, w_out[:, :], b_rows[:, 1, :], g("ch_a"))
                m["ch_a_read",] = mm
                banks_p.freed[i] = dve.do(lambda e: e.tensor_tensor(x2[p2][:, :, :], bank[:, :].rearrange("t (b c) -> t b c", b=B), x1[p2][:, :, :], ALU.add),
                                          [mm, g("acc0", n - 2), g("x2_ch", n - 2)])
                m["x2", n] = layer_norm(x2[p2], x2[p2][:, :, :], stats, mv, rstd, banks_p.freed[i], None, gb=0)
            return [in_proj(b) for b in range(B)] + [scores(s) for s in range(B)] + [softmax] + [context(s) for s in range(B)] + [out_proj]

        def gate(n):
            p2 = n % 2

            def logits():
                _, m["x2_ch", n] = transpose4(banks_p, x2[p2], ch_x[p2][:, :, :], g("x2", n), g("moe_up", n - 2))
                i, bank, freed = banks_p.take()
                for b in range(B):
                    mm = (pe.do if b == B - 1 else pe.part)(
                        lambda e, b=b: e.matmul(bank[:, b * NE:(b + 1) * NE], ch_x[p2][:, b, :], w_gate[:, :], start=True, stop=True), [g("x2_ch", n), freed])
                banks_p.freed[i] = dve.do(lambda e: e.tensor_tensor(logit[:, :, :], bank[:, 0:B * NE].rearrange("t (b x) -> t b x", b=B),
                                                                    b_gate[:, :].unsqueeze(1).to_broadcast([T, B, NE]), ALU.add), [mm])
                m["logit",] = banks_p.freed[i]

            def select():
                bc = lmax[:, :].unsqueeze(2).to_broadcast([T, B, NE])
                lg = logit[:, :, :]
                x = dve.do(lambda e: e.tensor_reduce(lmax[:, :], lg, AX.X, ALU.max), [g("logit")])
                x = dve.do(lambda e: e.tensor_tensor(lg, lg, bc, ALU.subtract), [x])
                x = act.do(lambda e: e.activation(lg, lg, ACT.Exp), [x])
                x = dve.do(lambda e: e.tensor_reduce(lmax[:, :], lg, AX.X, ALU.add), [x])
                x = dve.do(lambda e: e.reciprocal(lmax[:, :], lmax[:, :]), [x])
                p = dve.do(lambda e: e.tensor_tensor(lg, lg, bc, ALU.mult), [x])
                lcmp = tok_tmp[0][:, :, 0:NE * NE].rearrange("t b (i j) -> t b i j", i=NE)
                lcmp2 = tok_tmp[1][:, :, 0:NE * NE].rearrange("t b (i j) -> t b i j", i=NE)
                for b in range(B):
                    pj = logit[:, b, :].unsqueeze(1).to_broadcast([T, NE, NE])
                    pi = logit[:, b, :].unsqueeze(2).to_broadcast([T, NE, NE])
                    dve.do(lambda e, b=b, pj=pj, pi=pi: e.tensor_tensor(lcmp[:, b, :, :], pj, pi, ALU.is_gt), [p, g("tmp_free", 0), g("tmp_free", 1)])
                    x = dve.do(lambda e, b=b, pj=pj, pi=pi: e.tensor_tensor(lcmp2[:, b, :, :], pj, pi, ALU.is_equal), [p])
                x = dve.do(lambda e: e.tensor_tensor(tok_tmp[1][:, :, 0:NE * NE], tok_tmp[1][:, :, 0:NE * NE],
                                                     tril[:, :, :].rearrange("t i j -> t (i j)").unsqueeze(1).to_broadcast([T, B, NE * NE]), ALU.mult), [x])
                x = dve.do(lambda e: e.tensor_tensor(tok_tmp[0][:, :, 0:NE * NE], tok_tmp[0][:, :, 0:NE * NE], tok_tmp[1][:, :, 0:NE * NE], ALU.add), [x])
                x = dve.do(lambda e: e.tensor_reduce(rank[:, :, :], lcmp, AX.X, ALU.add), [x])
                m["tmp_free", 0] = m["tmp_free", 1] = x
                x = dve.do(lambda e: e.scalar_tensor_tensor(lg, rank[:, :, :], 1.5, lg, ALU.is_lt, ALU.mult), [x])
                x = dve.do(lambda e: e.tensor_reduce(lmax[:, :], lg, AX.X, ALU.add), [x])
                x = dve.do(lambda e: e.reciprocal(lmax[:, :], lmax[:, :]), [x])
                m["combine", n] = dve.do(lambda e: e.tensor_tensor(combine[p2][:, :, :], lg, bc, ALU.mult), [x, g("moe", n - 2)])

            def combine_ch():
                i, bank, freed = banks_p.take()
                for b in range(B):
                    tr = (pe.do if b == B - 1 else pe.part)(
                        lambda e, b=b: e.transpose(bank[0:NE, b * T:(b + 1) * T], combine[p2][:, b, :], ident[:, :]), [g("combine", n), freed])
                banks_p.freed[i] = act.do(lambda e: e.activation(combine_t[p2][:, :, :].rearrange("x b t -> x (b t)"), bank[0:NE, :], ACT.Copy),
                                          [tr, g("acc0", n - 2)])
                m["combine_t", n] = banks_p.freed[i]
            return [logits, select, combine_ch]

        def experts(n):
            p2 = n % 2

            def start():
                i, bank, freed = banks_y.take()
                for b in range(B):
                    mm = (pe.do if b == B - 1 else pe.part)(
                        lambda e, b=b: e.matmul(bank[:, b * C:(b + 1) * C], combine_t[p2][:, b, :], b2[:, :], start=True, stop=True),
                        [g("combine_t", n), freed, moe_loaded])
                banks_y.freed[i] = dve.do(lambda e: e.tensor_tensor(moe_acc[:, :, :], bank[:, :].rearrange("t (b c) -> t b c", b=B), x2[p2][:, :, :], ALU.add),
                                          [mm, g("x2", n)])
                m["acc0", n] = m["acc",] = banks_y.freed[i]

            def up(x, f):
                def run():
                    i, bank, freed = banks_h.take()
                    mm = pe.do(lambda e: e.matmul(bank[:, :], w1[:, x, f * 128:(f + 1) * 128], ch_x[p2][:, :, :].rearrange("c b t -> c (b t)"),
                                                  start=True, stop=True), [g("x2_ch", n), freed, moe_loaded])
                    slot = (x % 2) * FT + f
                    banks_h.freed[i] = act.do(lambda e: e.activation(hidden[:, slot, :], bank[:, :], ACT.Relu, bias=b1[:, x, f:f + 1]),
                                              [mm, g("down", x % 2)])
                    m["hidden", slot] = banks_h.freed[i]
                    if x == NE - 1 and f == FT - 1:
                        m["moe_up", n] = mm
                return run

            def down(x):
                def run():
                    i, bank, freed = banks_y.take()
                    for b in range(B):
                        for f in range(FT):
                            slot = (x % 2) * FT + f
                            mm = (pe.do if b == B - 1 and f == FT - 1 else pe.part)(
                                lambda e, b=b, f=f, slot=slot: e.matmul(bank[:, b * C:(b + 1) * C], hidden[:, slot, b * T:(b + 1) * T], w2[:, x, f, :],
                                                                        start=f == 0, stop=f == FT - 1), [g("hidden", slot), freed])
                    m["down", x % 2] = mm
                    for b in range(B):
                        ac = dve.do(lambda e, b=b: e.scalar_tensor_tensor(moe_acc[:, b, :], bank[:, b * C:(b + 1) * C], combine[p2][:, b, x:x + 1],
                                                                          moe_acc[:, b, :], ALU.mult, ALU.add), [mm, g("acc")])
                    banks_y.freed[i] = ac
                    m["acc",] = ac
                    if x == NE - 1:
                        m["moe", n] = ac
                return run

            def finish():
                y = layer_norm(moe_acc, moe_acc[:, :, :], stats_m, mv_m, rstd_m, g("acc"), None, gb=2)
                y = pool.do(lambda e: e.tensor_tensor(y_out[:, :, :], moe_acc[:, :, :], x1[p2][:, :, :], ALU.add), [y, g("stored", n - 1)])
                y = layer_norm(y_out, y_out[:, :, :], stats_m, mv_m, rstd_m, y, None)
                m["final", n] = y
                m["stored", n] = sp.dma(lambda e: e.dma_start(io["out"][:, n * T:(n + 1) * T, :].rearrange("b t c -> t b c"), y_out[:, :, :]),
                                        s_y[p2], [y])
            steps = [start] + [up(0, f) for f in range(FT)]
            for x in range(NE):
                if x + 1 < NE:
                    steps += [up(x + 1, f) for f in range(FT)]
                steps.append(down(x))
            return steps + [finish]

        mix, read, rule, prep, feed, moe = [], [], [], [], prologue, []
        feed += record(project(0)[0] + project(1)[0] + project(0)[1] + conv_norm(0))
        for i in range(NBLK + 2):
            if 0 <= i - 1 < NBLK:
                read += record(read_out(i - 1))
                mix += record(mixer_out(i - 1) + attention(i - 1) + gate(i - 1))
            if i < NBLK:
                prep += record(prepare(i))
                rule += record(chunks(i))
            if i + 1 < NBLK:
                feed += record((project(i + 2)[0] if i + 2 < NBLK else []) + project(i + 1)[1] + conv_norm(i + 1))
            if 0 <= i - 2 < NBLK:
                moe += record(experts(i - 2))
        moe += record([lambda: sp.wait(m["stored", NBLK - 1])])
        interleave([read, prep, mix, feed, moe, rule])

        names = [q.name for q in (pe, dve, act, pool, s_first, s_const, s_moe, *s_x, *s_xt, *s_y)]
        sems = {name: ctx.enter_context(nc.semaphore(name)) for name in names}
        block = ctx.enter_context(nc.Block())

        @block.tensor
        def _(eng):
            pe.emit(eng, sems)

        @block.vector
        def _(eng):
            dve.emit(eng, sems)

        @block.scalar
        def _(eng):
            act.emit(eng, sems)

        @block.gpsimd
        def _(eng):
            pool.emit(eng, sems)

        @block.sync
        def _(eng):
            sp.emit(eng, sems)


def kernel(**inputs):
    import concourse.bacc as bacc
    from concourse.bass_utils import run_bass_kernel_spmd

    a = {k[3:]: np.asarray(v) for k, v in inputs.items()}
    x = a["attn_x"]

    def rows(v):
        return np.tile(v[None], (128,) + (1,) * v.ndim)

    halves = 2
    arrays = {
        "x": x,
        "x_ch": x.reshape(B, NBLK, T, C).transpose(3, 1, 0, 2),
        "w_qkv": np.stack([a["attn_Wq"].T, a["attn_Wk"].T, a["attn_Wv"].T], 1),
        "b_qkv": np.stack([a["attn_bq"], a["attn_bk"], a["attn_bv"]], 1),
        "w_gates": np.concatenate([a["attn_Wa"].T, a["attn_Wb"].T], 1),
        "b_gates": np.stack([np.tile(np.repeat(v, halves), B) for v in (a["attn_ba"], a["attn_bb"])], 1),
        "w_conv": np.stack([a["attn_conv_q"][:, 0], a["attn_conv_k"][:, 0], a["attn_conv_v"][:, 0]], 1),
        "w_o": a["attn_Wo"].T,
        "b_rows": np.stack([a["attn_bo"], a["ffn_out_b"]])[None],
        "w_in": a["ffn_in_proj_w"].T,
        "b_in": rows(a["ffn_in_proj_b"]),
        "w_out": a["ffn_out_w"].T,
        "w_gate": a["ffn_gate_w"].T,
        "b_gate": rows(a["ffn_gate_b"]),
        "w1": a["ffn_w1"].transpose(2, 0, 1),
        "b1": a["ffn_b1"].reshape(NE, FT, 128).transpose(2, 0, 1),
        "w2": a["ffn_w2"].reshape(NE, C, FT, 128).transpose(3, 0, 2, 1),
        "b2": a["ffn_b2"],
        "ln_gb": rows(np.stack([a["ffn_ln1_g"], a["ffn_ln1_b"], a["ffn_ln2_g"], a["ffn_ln2_b"]])),
        "ident": np.eye(128, dtype=np.float32),
        "fold": np.repeat(np.eye(B * H, dtype=np.float32), halves, axis=0),
        "tril": np.tile(np.tril(np.ones((NE, NE), np.float32), -1)[None], (128, 1, 1)),
    }
    arrays = {k: np.ascontiguousarray(v) for k, v in arrays.items()}
    nc = bacc.Bacc("TRN2", target_bir_lowering=False, num_devices=1)
    io = {k: nc.dram_tensor(f"in_{k}", v.shape, F32, kind="ExternalInput").ap() for k, v in arrays.items()}
    io["out"] = nc.dram_tensor("out", (B, N, C), F32, kind="ExternalOutput").ap()
    build(nc, io)
    r = run_bass_kernel_spmd(nc, [{f"in_{k}": v for k, v in arrays.items()}], core_ids=[0])
    return r.results[0]["out"]
```
